# Optimizing a Trainium2 kernel written in Bass

```python
import numpy as np
import jax
import jax.numpy as jnp

def _softmax(x, axis=-1):
    return jax.nn.softmax(x, axis=axis)

def _gelu(x):
    return jax.nn.gelu(x, approximate=True)

def _silu(x):
    return jax.nn.silu(x)

def _sigmoid(x):
    return jax.nn.sigmoid(x)

def _layernorm(x, axis=-1, eps=1e-05):
    m = jnp.mean(x, axis=axis, keepdims=True)
    v = jnp.var(x, axis=axis, keepdims=True)
    return (x - m) / jnp.sqrt(v + eps)

def _scatter_add(tgt, idx, src, axis=0):
    return tgt.at[idx].add(src)

def _segment_sum(src, seg, n):
    return jax.ops.segment_sum(src, seg, n)
kernel_name = 'mk_conv_seq_d2_conv_nchw512_r4_27cdda'

def setup_inputs(seed: int=0):
    np.random.seed(seed)
    _w = jnp.asarray

    def _rec_inputs():
        import jax
        import jax.numpy as jnp
        _gk = jax.random.key(seed)
        x = 7.22e-05 + 1 * jax.random.normal(jax.random.fold_in(_gk, 1), (4, 128, 16, 16), jnp.float32)
        return x
    x = _rec_inputs()

    def _L0_conv_setup():
        import jax, jax.numpy as jnp
        import numpy as np
        DIM = 8
        EPS = 1e-15
        GROUPS_PW = 48

        def _conv(x, w, groups=1, pad=0):
            return jax.lax.conv_general_dilated(x, w, window_strides=(1, 1), padding=[(pad, pad), (pad, pad)], dimension_numbers=('NCHW', 'OIHW', 'NCHW'), feature_group_count=groups)
        key = jax.random.key(seed)
        k0, k1, k2, k3, k4 = jax.random.split(key, 5)
        B, C, H, W = (4, 128, 16, 16)
        td = 128
        x = jax.random.normal(k0, (B, C, H, W), jnp.float32)
        w_qkv = jax.random.normal(k1, (3 * td, C, 1, 1), jnp.float32) * 0.05
        w_dw = jax.random.normal(k2, (3 * td, 1, 5, 5), jnp.float32) * 0.05
        w_pw = jax.random.normal(k3, (3 * td, 3 * td // GROUPS_PW, 1, 1), jnp.float32) * 0.05
        w_proj = jax.random.normal(k4, (C, 2 * td, 1, 1), jnp.float32) * 0.05
        return {'x': x, 'w_qkv': w_qkv, 'w_dw': w_dw, 'w_pw': w_pw, 'w_proj': w_proj}
    _L0_conv_all = _L0_conv_setup()
    _L0_conv_in = {k: v for k, v in _L0_conv_all.items() if k in ('w_qkv', 'w_dw', 'w_pw', 'w_proj')}
    del _L0_conv_all

    def _L1_conv_setup():
        import jax, jax.numpy as jnp
        import numpy as np
        N, C, H, W = (32, 128, 32, 32)
        D = C // 2

        def _conv1x1(x, Wt, bt):
            return jnp.einsum('nchw,oc->nohw', x, Wt) + bt[None, :, None, None]
        key = jax.random.key(seed)
        ks = jax.random.split(key, 7)
        s = 0.05
        return {'x': jax.random.normal(ks[0], (N, C, H, W), jnp.float32), 'W_theta': jax.random.normal(ks[1], (D, C), jnp.float32) * s, 'b_theta': jax.random.normal(ks[2], (D,), jnp.float32) * s, 'W_phi': jax.random.normal(ks[3], (D, C), jnp.float32) * s, 'b_phi': jax.random.normal(ks[4], (D,), jnp.float32) * s, 'W_fuse': jax.random.normal(ks[5], (C, C), jnp.float32) * s, 'b_fuse': jax.random.normal(ks[6], (C,), jnp.float32) * s}
    _L1_conv_all = _L1_conv_setup()
    _L1_conv_in = {k: v for k, v in _L1_conv_all.items() if k in ('W_theta', 'b_theta', 'W_phi', 'b_phi', 'W_fuse', 'b_fuse')}
    del _L1_conv_all
    return {'x': x, 'L0_conv_w_qkv': _L0_conv_in['w_qkv'], 'L0_conv_w_dw': _L0_conv_in['w_dw'], 'L0_conv_w_pw': _L0_conv_in['w_pw'], 'L0_conv_w_proj': _L0_conv_in['w_proj'], 'L1_conv_W_theta': _L1_conv_in['W_theta'], 'L1_conv_b_theta': _L1_conv_in['b_theta'], 'L1_conv_W_phi': _L1_conv_in['W_phi'], 'L1_conv_b_phi': _L1_conv_in['b_phi'], 'L1_conv_W_fuse': _L1_conv_in['W_fuse'], 'L1_conv_b_fuse': _L1_conv_in['b_fuse']}

def reference(x, L0_conv_w_qkv, L0_conv_w_dw, L0_conv_w_pw, L0_conv_w_proj, L1_conv_W_theta, L1_conv_b_theta, L1_conv_W_phi, L1_conv_b_phi, L1_conv_W_fuse, L1_conv_b_fuse):
    import jax
    import jax.numpy as jnp

    def _L0_conv_ref(x, w_qkv, w_dw, w_pw, w_proj):
        import jax, jax.numpy as jnp
        import numpy as np
        DIM = 8
        EPS = 1e-15
        GROUPS_PW = 48

        def _conv(x, w, groups=1, pad=0):
            return jax.lax.conv_general_dilated(x, w, window_strides=(1, 1), padding=[(pad, pad), (pad, pad)], dimension_numbers=('NCHW', 'OIHW', 'NCHW'), feature_group_count=groups)
        qkv = _conv(x, w_qkv)
        agg = _conv(_conv(qkv, w_dw, groups=w_dw.shape[0], pad=2), w_pw, groups=GROUPS_PW)
        qkv = jnp.concatenate([qkv, agg], axis=1)
        B, _, H, W = qkv.shape
        qkv = qkv.reshape(B, -1, 3 * DIM, H * W)
        q = jax.nn.relu(qkv[:, :, :DIM])
        k = jax.nn.relu(qkv[:, :, DIM:2 * DIM])
        v = qkv[:, :, 2 * DIM:]
        v = jnp.pad(v, ((0, 0), (0, 0), (0, 1), (0, 0)), constant_values=1.0)
        vk = jnp.einsum('bhdn,bhen->bhde', v, k)
        out = jnp.einsum('bhde,bhen->bhdn', vk, q)
        out = out[:, :, :-1] / (out[:, :, -1:] + EPS)
        out = out.reshape(B, -1, H, W)
        return x + _conv(out, w_proj)

    def _L1_conv_ref(x, W_theta, b_theta, W_phi, b_phi, W_fuse, b_fuse):
        import jax, jax.numpy as jnp
        import numpy as np
        N, C, H, W = (32, 128, 32, 32)
        D = C // 2

        def _conv1x1(x, Wt, bt):
            return jnp.einsum('nchw,oc->nohw', x, Wt) + bt[None, :, None, None]
        n, c, h, w = x.shape
        theta = _conv1x1(x, W_theta, b_theta)
        phi = _conv1x1(x, W_phi, b_phi)
        d = theta.shape[1]
        hw = h * w
        t = theta.reshape(n, d, hw)
        p = phi.reshape(n, d, hw)
        g = x.reshape(n, c, hw)
        scale = 1.0 / np.sqrt(float(d))
        f = jnp.einsum('ndq,ndk->nqk', t, p) * scale
        f = jax.nn.softmax(f, axis=-1)
        attn = jnp.einsum('nqk,nck->ncq', f, g).reshape(n, c, h, w)
        return x + _conv1x1(attn, W_fuse, b_fuse)

    def _gn(v, G=32, eps=1e-05):
        B_, C_, H_, W_ = v.shape
        g = v.reshape(B_, G, C_ // G, H_, W_)
        m = jnp.mean(g, axis=(2, 3, 4), keepdims=True)
        s = jnp.var(g, axis=(2, 3, 4), keepdims=True)
        return ((g - m) / jnp.sqrt(s + eps)).reshape(v.shape)

    def _ln_c(v, eps=1e-06):
        m = jnp.mean(v, axis=1, keepdims=True)
        s = jnp.var(v, axis=1, keepdims=True)
        return (v - m) / jnp.sqrt(s + eps)

    def _ln_t(v, eps=1e-05):
        m = jnp.mean(v, axis=-1, keepdims=True)
        s = jnp.var(v, axis=-1, keepdims=True)
        return (v - m) / jnp.sqrt(s + eps)

    def _to_tokens(v):
        B_, C_, H_, W_ = v.shape
        return v.reshape(B_, C_, H_ * W_).transpose(0, 2, 1)

    def _from_tokens(t, like):
        B_, C_, H_, W_ = like.shape
        return t.transpose(0, 2, 1).reshape(B_, C_, H_, W_)
    x = _L0_conv_ref(x, L0_conv_w_qkv, L0_conv_w_dw, L0_conv_w_pw, L0_conv_w_proj)
    x = _L1_conv_ref(x, L1_conv_W_theta, L1_conv_b_theta, L1_conv_W_phi, L1_conv_b_phi, L1_conv_W_fuse, L1_conv_b_fuse)
    return x

_drawn_inputs = setup_inputs


def setup_inputs(seed=0):
    import zlib

    import numpy as np

    out = dict(_drawn_inputs(seed))
    spreads = {}
    factors = {'L0_conv_w_dw': 8.0,
     'L0_conv_w_pw': 8.0,
     'L1_conv_W_theta': 2.846,
     'L1_conv_b_theta': 8.0,
     'L1_conv_W_phi': 2.85,
     'L1_conv_b_phi': 8.0}
    for name, (base, spread) in spreads.items():
        noise = np.random.default_rng([zlib.crc32(name.encode()), seed]).standard_normal(out[name].shape)
        drawn = base * np.exp(spread * noise) if base else spread * noise
        out[name] = jnp.asarray(drawn.astype(out[name].dtype))
    for name, factor in factors.items():
        out[name] = (out[name] * factor).astype(out[name].dtype)
    return out
```

```python
from contextlib import ExitStack

import numpy as np

import concourse.bass as bass
from concourse import mybir

F32 = mybir.dt.float32
ALU = mybir.AluOpType
ACT = mybir.ActivationFunctionType
AX_X = mybir.AxisListType.X

P = 128
B, C, H, W = 4, 128, 16, 16
N = H * W
E = 8
HEADS = 16
KINDS = 3
GROUPS = HEADS * KINDS
TAPS = 5
HP, WP = H // 2, W // 2
PR, PCOL = HP + 2, WP + 2
ROW = B * PCOL
PLANE = PR * ROW
WIN = 3
SLOT = HP * ROW
KROWS = WIN * 4 * E
NPIX = B * HP * WP
D = 64
EPS = 1e-15
Q, K, V = 0, 1, 2
ORDER = (K, V, Q)
GPAD = (TAPS + 1) * TAPS + 2
GLEN = GPAD + GROUPS * TAPS * TAPS + 8


def shape_constants():
    p = np.arange(P)[:, None]
    m = np.arange(P)[None, :]
    same0 = p % HEADS == m % HEADS
    same1 = p // E == m // E
    cross = p // E == m % HEADS
    gather = p == m % 32 // E * 32 + m // 32 * E + m % E
    pick0 = (p % 32 < HEADS) & (p % HEADS == m % HEADS)
    pick1 = (p % 2 == 0) & (p % 32 // 2 == m // E)
    u, py, px = p // 32, p // 16 % 2, p // 8 % 2
    valid = []
    for v in range(WIN):
        for aa, bb in ((0, 0), (0, 1), (1, 0), (1, 1)):
            dy = 2 * u + py - (1 - aa)
            dx = 2 * v + px - (1 - bb)
            valid.append((dy >= 0) & (dy < TAPS) & (dx >= 0) & (dx < TAPS))
    parts = [same0, same1, pick0, pick1, cross, gather, *valid]
    return np.concatenate([np.asarray(a, np.float32) for a in parts], axis=1)


def conv_attention_kernel(nc, x, w_qkv, w_dw, w_pw, w_proj, w_theta, b_theta, w_phi, b_phi,
                          w_fuse, b_fuse, ident_in, const_in, out):
    with ExitStack() as ctx:
        def sb(name, *shape):
            return ctx.enter_context(nc.sbuf_tensor(name, list(shape), F32))

        def sem(name):
            return ctx.enter_context(nc.semaphore(name))

        xs = sb("xs", P, B, N)
        wqkv_n = sb("wqkv_n", P, KINDS, C)
        wpw_n = sb("wpw_n", P, KINDS, E)
        wproj_n = sb("wproj_n", P, 2 * P)
        wfuse_n = sb("wfuse_n", P, C)
        wth_n = sb("wth_n", D, C)
        wph_n = sb("wph_n", D, C)
        bth = sb("bth", D, 1)
        bph = sb("bph", D, 1)
        bfu = sb("bfu", P, 1)
        ident = sb("ident", P, P)
        consts = sb("consts", P, 6 * P + 4 * WIN)
        same = [consts[:, 0:P], consts[:, P:2 * P]]
        pick = consts[:, 2 * P:4 * P].rearrange("p (a m) -> p a m", a=2)
        pick_b = sb("pick_b", P, B, 2, P)
        cross, gather = consts[:, 4 * P:5 * P], consts[:, 5 * P:6 * P]
        valid = consts[0:KROWS, 6 * P:6 * P + 4 * WIN]
        ones = sb("ones", P, 32)
        wqkv_t = sb("wqkv_t", P, KINDS, P)
        wpw_r = sb("wpw_r", P, KINDS, WIN * 4, E)
        wpw_t = sb("wpw_t", KROWS, GROUPS * E)
        wproj_t = sb("wproj_t", P, 2, P)
        wfuse_t = sb("wfuse_t", P, C)
        wth_t = sb("wth_t", P, D)
        wph_t = sb("wph_t", P, D)
        taps = sb("taps", KROWS, GLEN)
        wsel = sb("wsel", KROWS, GROUPS, 4 * WIN)
        wconv = sb("wconv", KROWS, KINDS, HEADS, 4 * WIN, E)
        planes = sb("planes", P, KINDS, 4, PLANE)
        slots = sb("slots", KROWS, KINDS, HEADS, SLOT)
        rq = [sb(f"rq{a}", P, B, N) for a in range(2)]
        kt0 = sb("kt0", P, B, 2, P)
        vt0 = sb("vt0", P, B, 2, P)
        conv = sb("conv", P, KINDS, 4, NPIX)
        kt1 = sb("kt1", P, 2, 4, P)
        vt1 = sb("vt1", P, 2, 4, P)
        vk = [sb(f"vk{a}", P, B, P) for a in range(2)]
        ks = [sb(f"ks{a}", P, B, 32) for a in range(2)]
        m2 = [sb(f"m2{a}", P, B, P) for a in range(2)]
        den = [sb(f"den{a}", P, N) for a in range(2)]
        rden = [sb(f"rden{a}", P, N) for a in range(2)]
        qs = [sb(f"qs{a}", P, B, N) for a in range(2)]
        x1 = sb("x1", P, B, N)
        theta = sb("theta", D, B, N)
        phi = sb("phi", D, B, N)
        gf = sb("gf", P, B, 2, C)
        mx = sb("mx", P, B, 2)
        nmx = sb("nmx", P, B, 2)
        rs = sb("rs", P, B, 2)
        rrs = sb("rrs", P, B, 2)
        pn = sb("pn", P, B, 2, N)
        spare = planes[:, :, :, :].rearrange("p k a l -> p (k a l)")
        pr = spare[:, 0:2 * B * N].rearrange("p (b q n) -> p b q n", b=B, q=2)
        pt = spare[:, 2 * B * N:4 * B * N].rearrange("p (b k n) -> p b k n", b=B, k=2)
        ys = kt0[:, :, :, :].rearrange("p b t c -> p b (t c)")

        bank = [ctx.enter_context(nc.psum_tensor(f"bank{i}", [P, 512], F32)) for i in range(8)]

        taps_d = nc.dram_tensor("taps_d", [E, GROUPS * TAPS * TAPS], F32, kind="Internal").ap()
        planes_d = [nc.dram_tensor(f"planes_d{k}", [4, P, PLANE], F32, kind="Internal").ap()
                    for k in range(KINDS)]

        ld_ident, ld_wqkv, ld_x, ld_const = sem("ld_ident"), sem("ld_wqkv"), sem("ld_x"), sem("ld_const")
        ld_wpw, ld_wproj, ld_wl1, ld_bias = sem("ld_wpw"), sem("ld_wproj"), sem("ld_wl1"), sem("ld_bias")
        taps_in_dram, ld_taps = sem("taps_in_dram"), sem("ld_taps")
        planes_in_dram = [sem(f"planes_in_dram{k}") for k in range(KINDS)]
        ld_slots = [sem(f"ld_slots{k}") for k in range(KINDS)]
        stored = sem("stored")
        border_zero, taps_zero, ones_set = sem("border_zero"), sem("taps_zero"), sem("ones_set")
        pick_zero, pick_set = sem("pick_zero"), sem("pick_set")
        wconv_pool, wconv_dve, wsel_done = sem("wconv_pool"), sem("wconv_dve"), sem("wsel_done")
        wt_mm, wt_out = sem("wt_mm"), sem("wt_out")
        wpw_copied = sem("wpw_copied")
        wpw_mm, wpw_out = sem("wpw_mm"), sem("wpw_out")
        wpr_mm, wpr_out = sem("wpr_mm"), sem("wpr_out")
        wl1_mm, wl1_out = sem("wl1_mm"), sem("wl1_out")
        nat_mm, nat_act, nat_dve = sem("nat_mm"), sem("nat_act"), sem("nat_dve")
        rq0_act, rq0_dve = sem("rq0_act"), sem("rq0_dve")
        tok_mm, kt0_out, vt0_out = sem("tok_mm"), sem("kt0_out"), sem("vt0_out")
        vk_mm = [sem(f"vk_mm{a}") for a in range(2)]
        vk_out = [sem(f"vk_out{a}") for a in range(2)]
        den_mm = [sem(f"den_mm{a}") for a in range(2)]
        den_out = [sem(f"den_out{a}") for a in range(2)]
        rden_out = [sem(f"rden_out{a}") for a in range(2)]
        m2_mm = [sem(f"m2_mm{a}") for a in range(2)]
        m2_out = [sem(f"m2_out{a}") for a in range(2)]
        bc_mm = [sem(f"bc_mm{a}") for a in range(2)]
        qs_out = [sem(f"qs_out{a}") for a in range(2)]
        conv_mm, conv_act, conv_dve = sem("conv_mm"), sem("conv_act"), sem("conv_dve")
        tr_k_mm, tr_v_mm, kt1_out, vt1_out = sem("tr_k_mm"), sem("tr_v_mm"), sem("kt1_out"), sem("vt1_out")
        natq_mm, rq1_act, rq1_dve = sem("natq_mm"), sem("rq1_act"), sem("rq1_dve")
        proj_mm, x1_out = sem("proj_mm"), sem("x1_out")
        tf_mm, tf_out = sem("tf_mm"), sem("tf_out")
        f_mm, mx_out, nmx_out, exp_out = sem("f_mm"), sem("mx_out"), sem("nmx_out"), sem("exp_out")
        rrs_out, pn_out = sem("rrs_out"), sem("pn_out")
        pt_mm, pt_out = sem("pt_mm"), sem("pt_out")
        y_mm, y_out = sem("y_mm"), sem("y_out")

        def parity(t, py, px, order="y b x"):
            v = t[:, :, :].rearrange(f"c b (y p x q) -> c p q {order}", p=2, q=2, y=HP, x=WP)
            return v[:, py, px]

        def split(i, order="y b x"):
            return bank[i][:, :].rearrange(f"c (q {order}) -> c q {order}", q=2, b=B, y=HP, x=WP)

        def conv_weights(kind):
            sel = wsel[:, :, :].rearrange("p (h k) w -> p k h w", k=KINDS)[:, kind]
            pw = wpw_t[:, :].rearrange("p (h k o) -> p k h o", k=KINDS, o=E)[:, kind]
            shape = [KROWS, HEADS, 4 * WIN, E]
            return (wconv[:, kind], sel.unsqueeze(3).broadcast_to(shape),
                    pw.unsqueeze(2).broadcast_to(shape))

        def plane_rows(kind, py):
            v = planes[:, kind, 2 * py:2 * py + 2, ROW:PLANE - ROW]
            return v.rearrange("c q (m x) -> c q m x", x=PCOL)[:, :, :, 1:1 + WP]

        def plane_bank(i, py):
            return bank[nat_bank(i, py)][:, :].rearrange("c (q m x) -> c q m x", q=2, x=WP)

        def nat_bank(i, py):
            return 4 + (2 * i + py) % 4

        def conv_bank(i, half):
            return (2 * i + half) % 4

        def conv_out(kind, half):
            return conv[:, kind, 2 * half:2 * half + 2, :].rearrange("p r n -> p (r n)")

        def tokens(t, pair):
            return t[:, 2 * pair:2 * pair + 2].rearrange("p b t c -> p (b t c)")

        def by_phase(t, pair):
            return t[:, pair].rearrange("p a (h e) -> p h a e", e=E)

        def tr_bank(i):
            return bank[i][:, :].rearrange("p (h a e) -> p h a e", a=4, e=E)

        block = ctx.enter_context(nc.Block())

        @block.sync
        def _(sp):
            sp.dma_start(wqkv_n[:, :, :], w_qkv.rearrange("(n p) c u v -> p n (c u v)", p=P)).then_inc(ld_wqkv, 16)
            sp.dma_start(ident[:, :], ident_in).then_inc(ld_ident, 16)
            sp.dma_start(xs[:, :, :], x.rearrange("b c h w -> c b (h w)")).then_inc(ld_x, 16)
            sp.dma_start(consts[:, :], const_in).then_inc(ld_const, 16)
            sp.dma_start(wproj_n[:, :], w_proj.rearrange("o c u v -> o (c u v)")).then_inc(ld_wproj, 16)
            for i, kind in enumerate(ORDER):
                sp.wait_ge(nat_act, i + 1)
                sp.wait_ge(nat_dve, i + 1)
                sp.wait_ge(border_zero, 2)
                sp.dma_start(planes_d[kind].rearrange("a p l -> p a l"),
                             planes[:, kind, :, :]).then_inc(planes_in_dram[kind], 16)
                if i == 0:
                    sp.dma_start(wfuse_n[:, :], w_fuse).then_inc(ld_wl1, 16)
                    sp.dma_start(wth_n[:, :], w_theta).then_inc(ld_wl1, 16)
                    sp.dma_start(wph_n[:, :], w_phi).then_inc(ld_wl1, 16)
                sp.wait_ge(planes_in_dram[kind], 16)
                for u in range(WIN):
                    src = planes_d[kind].rearrange("a (c g) l -> (a c) g l", c=E)
                    sp.dma_start(slots[32 * u:32 * (u + 1), kind, :, :],
                                 src[:, :, u * ROW:u * ROW + SLOT]).then_inc(ld_slots[kind], 16)
            for b in range(B):
                sp.wait_ge(y_out, b + 1)
                sp.dma_start(out[b].rearrange("c h w -> c (h w)"), ys[:, b, :]).then_inc(stored, 16)
            sp.wait_ge(stored, 16 * B)

        @block.gpsimd
        def _(pool):
            nc.gpsimd.memset(taps[:, 0:GPAD], 0.0).then_inc(taps_zero, 1)
            nc.gpsimd.memset(taps[:, GLEN - 40:GLEN], 0.0).then_inc(taps_zero, 1)
            nc.gpsimd.memset(ones[:, :], 1.0).then_inc(ones_set, 1)
            allp = planes[:, :, :, :].rearrange("c k a l -> c (k a) l")
            rows = allp.rearrange("c a (r l) -> c a r l", r=PR)
            nc.gpsimd.memset(rows[:, :, 0:PR:PR - 1, :], 0.0).then_inc(border_zero, 1)
            cols = allp[:, :, ROW:PLANE - ROW].rearrange("c a (m x) -> c a m x", x=PCOL)
            nc.gpsimd.memset(cols[:, :, :, 0:PCOL:PCOL - 1], 0.0).then_inc(border_zero, 1)
            nc.gpsimd.memset(pick_b[:, :, :, :], 0.0).then_inc(pick_zero, 1)
            pool.wait_ge(taps_zero, 2)
            pool.wait_ge(taps_in_dram, 16)
            for s in range(WIN * 4):
                u, py, px = s // 4, s // 2 % 2, s % 2
                at = GPAD - TAPS * (2 * u + py) - px
                pool.dma_start(taps[E * s:E * (s + 1), at:at + GROUPS * TAPS * TAPS], taps_d).then_inc(ld_taps, 16)
            pool.wait_ge(ld_const, 16)
            pool.wait_ge(pick_zero, 1)
            for b in range(B):
                rows = slice(32 * b, 32 * (b + 1))
                if b:
                    pool.wait_ge(pick_set, b)
                nc.gpsimd.tensor_copy(pick_b[rows, b], pick[rows]).then_inc(pick_set, 1)
            pool.wait_ge(pick_set, B)
            pool.wait_ge(wsel_done, 2)
            pool.wait_ge(wpw_out, 1)
            for kind in (V, Q):
                nc.gpsimd.tensor_tensor(*conv_weights(kind), ALU.mult).then_inc(wconv_pool, 1)

        @block.scalar
        def _(act):
            act.dma_start(wpw_n[:, :, :], w_pw.rearrange("(n p) c u v -> p n (c u v)", p=P)).then_inc(ld_wpw, 16)
            act.dma_start(taps_d.rearrange("c (g t) -> g c t", t=TAPS * TAPS),
                          w_dw.rearrange("(g c) o u v -> g c (o u v)", c=E)).then_inc(taps_in_dram, 16)
            act.dma_start(bth[:, :], b_theta.rearrange("(p o) -> p o", o=1)).then_inc(ld_bias, 16)
            act.dma_start(bph[:, :], b_phi.rearrange("(p o) -> p o", o=1)).then_inc(ld_bias, 16)
            act.dma_start(bfu[:, :], b_fuse.rearrange("(p o) -> p o", o=1)).then_inc(ld_bias, 16)
            act.wait_ge(ld_wpw, 16)
            nc.scalar.activation(wpw_r[:, :, :, :], wpw_n[:, :, :].unsqueeze(2).broadcast_to([P, KINDS, WIN * 4, E]),
                                 ACT.Copy).then_inc(wpw_copied, 1)
            for i, kind in enumerate(ORDER):
                act.wait_ge(nat_mm, 2 * i + 1)
                nc.scalar.activation(plane_rows(kind, 0), plane_bank(i, 0), ACT.Copy).then_inc(nat_act, 1)
            for px in range(2):
                nc.scalar.activation(parity(rq[0], 0, px), split(4)[:, px], ACT.Relu).then_inc(rq0_act, 1)
            for pair in range(2):
                act.wait_ge(tok_mm, 2 * pair + 1)
                nc.scalar.activation(tokens(kt0, pair), bank[6 - 2 * pair][:, :], ACT.Relu).then_inc(kt0_out, 1)
            act.wait_ge(m2_mm[0], 1)
            nc.scalar.activation(m2[0][:, :, :].rearrange("p b c -> p (b c)"), bank[5][:, :], ACT.Copy).then_inc(m2_out[0], 1)
            for i, kind in enumerate(ORDER):
                act.wait_ge(conv_mm, 2 * i + 1)
                nc.scalar.activation(conv_out(kind, 0), bank[conv_bank(i, 0)][:, :], ACT.Copy).then_inc(conv_act, 1)
                if kind == V:
                    for pair in range(2):
                        act.wait_ge(tr_k_mm, pair + 1)
                        nc.scalar.activation(by_phase(kt1, pair), tr_bank(4 + pair), ACT.Relu).then_inc(kt1_out, 1)
            act.wait_ge(natq_mm, 1)
            for bb in range(2):
                nc.scalar.activation(parity(rq[1], 1, 1 - bb, "b y x"), split(2, "b y x")[:, bb], ACT.Relu).then_inc(rq1_act, 1)
            act.wait_ge(m2_mm[1], 1)
            nc.scalar.activation(m2[1][:, :, :].rearrange("p b c -> p (b c)"), bank[7][:, :], ACT.Copy).then_inc(m2_out[1], 1)
            act.wait_ge(ld_bias, 48)

            def theta_phi(b):
                act.wait_ge(tf_mm, b + 1)
                src = bank[4 + b % 2]
                nc.scalar.activation(theta[:, b, :], src[0:D, 0:N], ACT.Identity, bias=bth[:, 0:1]).then_inc(tf_out, 1)
                nc.scalar.activation(phi[:, b, :], src[D:2 * D, 0:N], ACT.Identity, bias=bph[:, 0:1]).then_inc(tf_out, 1)
                nc.scalar.activation(gf[:, b].rearrange("p k c -> p (k c)"), src[:, N:2 * N], ACT.Copy).then_inc(tf_out, 1)

            def exponentials(b):
                act.wait_ge(nmx_out, b + 1)
                for qc in range(2):
                    nc.scalar.activation(pr[:, b, qc, :], bank[6 + b % 2][:, qc * N:(qc + 1) * N], ACT.Exp,
                                         bias=nmx[:, b, qc:qc + 1], scale=D ** -0.5,
                                         accum_out=rs[:, b, qc:qc + 1]).then_inc(exp_out, 1)

            theta_phi(0)
            theta_phi(1)
            exponentials(0)
            theta_phi(2)
            exponentials(1)
            theta_phi(3)
            exponentials(2)
            exponentials(3)

        @block.vector
        def _(dve):
            dve.wait_ge(wt_mm, 1)
            src = bank[0][:, 0:KINDS * P].rearrange("c (h k e) -> c k e h", k=KINDS, e=E)
            for kind in ORDER:
                nc.vector.tensor_copy(wqkv_t[:, kind].rearrange("c (e h) -> c e h", e=E), src[:, kind]).then_inc(wt_out, 1)
            for i, kind in enumerate(ORDER):
                dve.wait_ge(nat_mm, 2 * i + 2)
                nc.vector.tensor_copy(plane_rows(kind, 1), plane_bank(i, 1)).then_inc(nat_dve, 1)
                if i == 1:
                    dve.wait_ge(wpw_mm, 1)
                    nc.vector.tensor_copy(wpw_t[:, :], bank[1][0:KROWS, 0:GROUPS * E]).then_inc(wpw_out, 1)
            for px in range(2):
                nc.vector.tensor_scalar_max(parity(rq[0], 1, px), split(5)[:, px], 0.0).then_inc(rq0_dve, 1)
            dve.wait_ge(wpr_mm, 1)
            nc.vector.tensor_copy(wproj_t[:, :, :].rearrange("p a c -> p (a c)"), bank[2][:, 0:2 * P]).then_inc(wpr_out, 1)
            for pair in range(2):
                dve.wait_ge(tok_mm, 2 * pair + 2)
                nc.vector.tensor_copy(tokens(vt0, pair), bank[7 - 2 * pair][:, :]).then_inc(vt0_out, 1)
            dve.wait_ge(ld_taps, 16 * WIN * 4)
            dve.wait_ge(ld_const, 16)
            for aa in range(2):
                at = GPAD + TAPS * (aa - 1) - 1
                src = taps[:, at:at + GROUPS * TAPS * TAPS].rearrange("p (g t) -> p g t", t=TAPS * TAPS)[:, :, 0:2 * WIN]
                src = src.rearrange("p g (v b) -> p g v b", b=2)
                m = valid.rearrange("p (v a b) -> p a v b", a=2, b=2)[:, aa].unsqueeze(1).broadcast_to([KROWS, GROUPS, WIN, 2])
                dst = wsel[:, :, :].rearrange("p g (v a b) -> p a g v b", a=2, b=2)[:, aa]
                nc.vector.tensor_tensor(dst, src, m, ALU.mult).then_inc(wsel_done, 1)
            dve.wait_ge(wsel_done, 2)
            dve.wait_ge(wpw_out, 1)
            nc.vector.tensor_tensor(*conv_weights(K), ALU.mult).then_inc(wconv_dve, 1)

            def attend_sums(a, banks):
                for pair in range(2):
                    images = slice(2 * pair, 2 * pair + 2) if a == 0 else slice(pair, B, 2)
                    dve.wait_ge(vk_mm[a], pair + 1)
                    src = bank[banks[pair]][:, :].rearrange("p (b n) -> p b n", b=2)
                    mask = (cross, same[1])[a].unsqueeze(1).broadcast_to([P, 2, P])
                    nc.vector.tensor_tensor(vk[a][:, images, :], src[:, :, 0:P], mask, ALU.mult).then_inc(vk_out[a], 1)
                    cols = same[a][:, 0:32] if a == 0 else same[a].rearrange("p (h e) -> p h e", e=E)[:, :, 0:2]
                    for b in range(2):
                        o, s = ks[a][:, images, :][:, b], src[:, b, P:P + 32]
                        if a == 1:
                            o, s = (t.rearrange("p (h e) -> p h e", e=2) for t in (o, s))
                        nc.vector.tensor_tensor(o, s, cols, ALU.mult).then_inc(vk_out[a], 1)

            def reciprocals(a, i):
                dve.wait_ge(den_mm[a], 1)
                nc.vector.tensor_scalar_add(den[a][:, :], bank[i][:, 0:N], EPS).then_inc(den_out[a], 1)
                dve.wait_ge(den_out[a], 1)
                nc.vector.reciprocal(rden[a][:, :], den[a][:, :]).then_inc(rden_out[a], 1)

            def scale_q(a, banks):
                for pair in range(2):
                    dve.wait_ge(bc_mm[a], pair + 1)
                    o = qs[a][:, 2 * pair:2 * pair + 2, :].rearrange("p b n -> p (b n)")
                    q = rq[a][:, 2 * pair:2 * pair + 2, :].rearrange("p b n -> p (b n)")
                    nc.vector.tensor_tensor(o, bank[banks[pair]][:, :], q, ALU.mult).then_inc(qs_out[a], 1)

            attend_sums(0, (6, 7))
            dve.wait_ge(wl1_mm, 1)
            nc.vector.tensor_copy(wfuse_t[:, :], bank[3][:, 0:C]).then_inc(wl1_out, 1)
            nc.vector.tensor_copy(wth_t[:, :], bank[3][:, C:C + D]).then_inc(wl1_out, 1)
            nc.vector.tensor_copy(wph_t[:, :], bank[3][:, C + D:C + 2 * D]).then_inc(wl1_out, 1)
            reciprocals(0, 4)
            scaled = False
            for i, kind in enumerate(ORDER):
                dve.wait_ge(conv_mm, 2 * i + 2)
                nc.vector.tensor_copy(conv_out(kind, 1), bank[conv_bank(i, 1)][:, :]).then_inc(conv_dve, 1)
                if kind == K:
                    scale_q(0, (6, 7))
                if kind == Q:
                    pass
                if kind == V:
                    for pair in range(2):
                        dve.wait_ge(tr_v_mm, pair + 1)
                        nc.vector.tensor_copy(by_phase(vt1, pair), tr_bank(6 + pair)).then_inc(vt1_out, 1)
            attend_sums(1, (4, 5))
            dve.wait_ge(natq_mm, 2)
            for bb in range(2):
                nc.vector.tensor_scalar_max(parity(rq[1], 0, 1 - bb, "b y x"), split(3, "b y x")[:, bb], 0.0).then_inc(rq1_dve, 1)
            reciprocals(1, 6)
            scale_q(1, (0, 1))

            def first_layer(b):
                dve.wait_ge(proj_mm, b + 1)
                nc.vector.tensor_tensor(x1[:, b, :], bank[2 + b % 2][:, 0:N], xs[:, b, :], ALU.add).then_inc(x1_out, 1)

            def maxima(b):
                dve.wait_ge(f_mm, b + 1)
                nc.vector.tensor_reduce(mx[:, b, :], bank[6 + b % 2][:, :].rearrange("p (q n) -> p q n", q=2),
                                        AX_X, ALU.max).then_inc(mx_out, 1)
                dve.wait_ge(mx_out, b + 1)
                nc.vector.tensor_scalar_mul(nmx[:, b, :], mx[:, b, :], -D ** -0.5).then_inc(nmx_out, 1)

            def normalize(b):
                dve.wait_ge(exp_out, 2 * b + 2)
                nc.vector.reciprocal(rrs[:, b, :], rs[:, b, :]).then_inc(rrs_out, 1)
                dve.wait_ge(rrs_out, b + 1)
                for qc in range(2):
                    nc.vector.tensor_scalar_mul(pn[:, b, qc, :], pr[:, b, qc, :], rrs[:, b, qc:qc + 1]).then_inc(pn_out, 1)

            def transposed(b):
                dve.wait_ge(pt_mm, b + 1)
                nc.vector.tensor_copy(pt[:, b].rearrange("p k n -> p (k n)"), bank[b % 2][:, :]).then_inc(pt_out, 1)

            def result(b):
                dve.wait_ge(y_mm, b + 1)
                nc.vector.scalar_tensor_tensor(ys[:, b, :], bank[2 + b % 2][:, 0:N], bfu[:, 0:1], x1[:, b, :],
                                               ALU.add, ALU.add).then_inc(y_out, 1)

            dve.wait_ge(ld_bias, 48)
            for step, b in ((first_layer, 0), (first_layer, 1), (first_layer, 2), (maxima, 0), (first_layer, 3),
                            (maxima, 1), (normalize, 0), (maxima, 2), (normalize, 1), (transposed, 0), (maxima, 3),
                            (normalize, 2), (transposed, 1), (result, 0), (normalize, 3), (transposed, 2),
                            (result, 1), (transposed, 3), (result, 2), (result, 3)):
                step(b)

        @block.tensor
        def _(pe):
            pe.wait_ge(ld_wqkv, 16)
            pe.wait_ge(ld_ident, 16)
            for n in range(KINDS):
                last = nc.tensor.transpose(bank[0][:, n * P:(n + 1) * P], wqkv_n[:, n, :], ident[:, :])
            last.then_inc(wt_mm, 1)
            pe.wait_ge(ld_x, 16)

            def natural(i):
                kind = ORDER[i]
                pe.wait_ge(wt_out, i + 1)
                for py in range(2):
                    if i == 2:
                        pe.wait_ge((nat_act, nat_dve)[py], 1)
                    for px in range(2):
                        last = nc.tensor.matmul(bank[nat_bank(i, py)][:, px * NPIX:(px + 1) * NPIX],
                                                wqkv_t[:, kind, :], parity(xs, py, px), start=True, stop=True)
                    last.then_inc(nat_mm, 1)

            natural(0)
            natural(1)
            pe.wait_ge(wpw_copied, 1)
            for n in range(KINDS):
                src = wpw_r[:, n].rearrange("p s e -> p (s e)")
                last = nc.tensor.transpose(bank[1][0:KROWS, n * P:(n + 1) * P], src, ident[:, :])
            last.then_inc(wpw_mm, 1)
            natural(2)
            pe.wait_ge(ld_wproj, 16)
            nc.tensor.transpose(bank[2][:, 0:P], wproj_n[:, 0:P], ident[:, :])
            nc.tensor.transpose(bank[2][:, P:2 * P], wproj_n[:, P:2 * P], ident[:, :]).then_inc(wpr_mm, 1)
            for pair in range(2):
                for kind, free in ((K, nat_act if pair == 0 else rq0_act), (V, nat_dve if pair == 0 else rq0_dve)):
                    pe.wait_ge(free, 2)
                    dst = bank[(6 if kind == K else 7) - 2 * pair]
                    w = wqkv_t[:, kind, :]
                    if kind == V:
                        w = w.rearrange("c (e h) -> c h e", e=E)
                    for n in range(4):
                        b, t = 2 * pair + n // 2, n % 2
                        last = nc.tensor.matmul(dst[:, n * P:(n + 1) * P], xs[:, b, t * P:(t + 1) * P],
                                                w, start=True, stop=True)
                    last.then_inc(tok_mm, 1)
            pe.wait_ge(ones_set, 1)
            for pair in range(2):
                pe.wait_ge(kt0_out, pair + 1)
                pe.wait_ge(vt0_out, pair + 1)
                for s in range(2):
                    b, at = 2 * pair + s, 256 * s
                    for t in range(2):
                        nc.tensor.matmul(bank[6 + pair][:, at:at + P], vt0[:, b, t, :], kt0[:, b, t, :],
                                         start=t == 0, stop=t == 1)
                    for t in range(2):
                        last = nc.tensor.matmul(bank[6 + pair][:, at + P:at + P + 32], kt0[:, b, t, :], ones[:, :],
                                                start=t == 0, stop=t == 1)
                last.then_inc(vk_mm[0], 1)
            pe.wait_ge(ld_wl1, 48)
            nc.tensor.transpose(bank[3][:, 0:C], wfuse_n[:, :], ident[:, :])
            nc.tensor.transpose(bank[3][:, C:C + D], wth_n[:, :], ident[0:D, 0:D])
            nc.tensor.transpose(bank[3][:, C + D:C + 2 * D], wph_n[:, :], ident[0:D, 0:D]).then_inc(wl1_mm, 1)

            def denominators(a, i):
                pe.wait_ge(vk_out[a], 6)
                for b in range(B):
                    last = nc.tensor.matmul(bank[i][32 * b:32 * (b + 1), 0:N], ks[a][:, b, :], rq[a][:, b, :],
                                            start=True, stop=True)
                last.then_inc(den_mm[a], 1)

            def projected_sums(a, i):
                for b in range(B):
                    last = nc.tensor.matmul(bank[i][:, b * P:(b + 1) * P], vk[a][:, b, :], wproj_t[:, a, :],
                                            start=True, stop=True)
                last.then_inc(m2_mm[a], 1)

            def spread(a, pair, i):
                pe.wait_ge(rden_out[a], 1)
                pe.wait_ge(pick_set, B)
                for s in range(2):
                    b = 2 * pair + s
                    last = nc.tensor.matmul(bank[i][:, s * N:(s + 1) * N], pick_b[:, b, a, :], rden[a][:, :],
                                            start=True, stop=True)
                last.then_inc(bc_mm[a], 1)

            pe.wait_ge(rq0_act, 2)
            pe.wait_ge(rq0_dve, 2)
            pe.wait_ge(kt0_out, 2)
            denominators(0, 4)
            pe.wait_ge(wpr_out, 1)
            pe.wait_ge(vt0_out, 2)
            projected_sums(0, 5)

            def convolve(i, half):
                kind = ORDER[i]
                dst = bank[conv_bank(i, half)]
                for r in (2 * half, 2 * half + 1):
                    at = (r - 2 * half) * NPIX
                    for v in range(WIN):
                        for j in range(4):
                            h = 4 * r + j
                            w = wconv[:, kind, h, 4 * v:4 * (v + 1), :].rearrange("p a o -> p (a o)")
                            src = slots[:, kind, h, :].rearrange("p (y b x) -> p b y x", b=B, x=PCOL)[:, :, :, v:v + WP]
                            last = nc.tensor.matmul(dst[32 * j:32 * (j + 1), at:at + NPIX], w, src,
                                                    start=v == 0, stop=v == WIN - 1)
                last.then_inc(conv_mm, 1)

            def by_token(kind, pair, i, done):
                for r in range(4):
                    src = conv[:, kind, r, pair * P:(pair + 1) * P]
                    last = nc.tensor.transpose(bank[i][:, r * P:(r + 1) * P], src, ident[:, :])
                last.then_inc(done, 1)

            pe.wait_ge(ld_slots[K], 16 * WIN)
            pe.wait_ge(wconv_dve, 1)
            convolve(0, 0)
            pe.wait_ge(wpw_out, 1)
            convolve(0, 1)
            spread(0, 0, 6)
            spread(0, 1, 7)
            pe.wait_ge(ld_slots[V], 16 * WIN)
            pe.wait_ge(wconv_pool, 1)
            convolve(1, 0)
            pe.wait_ge(conv_act, 1)
            pe.wait_ge(conv_dve, 1)
            pe.wait_ge(den_out[0], 1)
            by_token(K, 0, 4, tr_k_mm)
            pe.wait_ge(m2_out[0], 1)
            by_token(K, 1, 5, tr_k_mm)
            pe.wait_ge(wl1_out, 3)
            convolve(1, 1)
            pe.wait_ge(ld_slots[Q], 16 * WIN)
            pe.wait_ge(wconv_pool, 2)
            convolve(2, 0)
            pe.wait_ge(conv_act, 2)
            pe.wait_ge(conv_dve, 2)
            pe.wait_ge(qs_out[0], 2)
            by_token(V, 0, 6, tr_v_mm)
            by_token(V, 1, 7, tr_v_mm)
            convolve(2, 1)
            pe.wait_ge(kt1_out, 2)
            pe.wait_ge(vt1_out, 2)
            for s in range(2):
                for pair in range(2):
                    at, rows = 256 * pair, slice(D * s, D * (s + 1))
                    for ph in range(4):
                        nc.tensor.matmul(bank[4 + s][:, at:at + P], vt1[rows, pair, ph, :], kt1[rows, pair, ph, :],
                                         start=ph == 0, stop=ph == 3)
                    for ph in range(4):
                        last = nc.tensor.matmul(bank[4 + s][:, at + P:at + P + 32], kt1[rows, pair, ph, :],
                                                ones[rows, :], start=ph == 0, stop=ph == 3)
                last.then_inc(vk_mm[1], 1)
            pe.wait_ge(conv_act, 3)
            pe.wait_ge(conv_dve, 3)
            for aa in range(2):
                for bb in range(2):
                    w = gather[:, 32 * (2 * aa + bb):32 * (2 * aa + bb + 1)]
                    for r in range(4):
                        last = nc.tensor.matmul(bank[2 + aa][32 * r:32 * (r + 1), bb * NPIX:(bb + 1) * NPIX], w,
                                                conv[:, Q, r, :], start=True, stop=True)
                last.then_inc(natq_mm, 1)
            pe.wait_ge(rq1_act, 2)
            pe.wait_ge(rq1_dve, 2)
            pe.wait_ge(vt1_out, 2)
            denominators(1, 6)
            projected_sums(1, 7)

            def project(b):
                if b >= 2:
                    pe.wait_ge(x1_out, b - 1)
                for a in range(2):
                    if a == 1:
                        pe.wait_ge(m2_out[1], 1)
                        pe.wait_ge(qs_out[1], b // 2 + 1)
                    last = nc.tensor.matmul(bank[2 + b % 2][:, 0:N], m2[a][:, b, :], qs[a][:, b, :],
                                            start=a == 0, stop=a == 1)
                last.then_inc(proj_mm, 1)

            def theta_phi_values(b):
                pe.wait_ge(x1_out, b + 1)
                if b >= 2:
                    pe.wait_ge(tf_out, 3 * (b - 1))
                dst = bank[4 + b % 2]
                nc.tensor.matmul(dst[0:D, 0:N], wth_t[:, :], x1[:, b, :], start=True, stop=True)
                nc.tensor.matmul(dst[D:2 * D, 0:N], wph_t[:, :], x1[:, b, :], start=True, stop=True)
                for kc in range(2):
                    last = nc.tensor.matmul(dst[:, N + kc * C:N + (kc + 1) * C], x1[:, b, kc * P:(kc + 1) * P],
                                            wfuse_t[:, :], start=True, stop=True)
                last.then_inc(tf_mm, 1)

            def scores(b):
                pe.wait_ge(tf_out, 3 * b + 2)
                if b >= 2:
                    pe.wait_ge(exp_out, 2 * (b - 1))
                for qc in range(2):
                    last = nc.tensor.matmul(bank[6 + b % 2][:, qc * N:(qc + 1) * N], theta[:, b, qc * P:(qc + 1) * P],
                                            phi[:, b, :], start=True, stop=True)
                last.then_inc(f_mm, 1)

            def transpose_probs(b):
                pe.wait_ge(pn_out, 2 * b + 2)
                if b >= 2:
                    pe.wait_ge(pt_out, b - 1)
                for kc in range(2):
                    for qc in range(2):
                        at = kc * N + qc * P
                        last = nc.tensor.transpose(bank[b % 2][:, at:at + P], pn[:, b, qc, kc * P:(kc + 1) * P], ident[:, :])
                last.then_inc(pt_mm, 1)

            def attend(b):
                pe.wait_ge(pt_out, b + 1)
                pe.wait_ge(tf_out, 3 * b + 3)
                pe.wait_ge(x1_out, 3 + b % 2)
                if b >= 2:
                    pe.wait_ge(y_out, b - 1)
                for kc in range(2):
                    last = nc.tensor.matmul(bank[2 + b % 2][:, 0:N], gf[:, b, kc, :], pt[:, b, kc, :],
                                            start=kc == 0, stop=kc == 1)
                last.then_inc(y_mm, 1)

            spread(1, 0, 0)
            spread(1, 1, 1)
            for step, b in ((project, 0), (project, 1), (theta_phi_values, 0), (project, 2), (theta_phi_values, 1),
                            (scores, 0), (project, 3), (theta_phi_values, 2), (scores, 1), (transpose_probs, 0),
                            (theta_phi_values, 3), (scores, 2), (transpose_probs, 1), (attend, 0), (scores, 3),
                            (transpose_probs, 2), (attend, 1), (transpose_probs, 3), (attend, 2), (attend, 3)):
                step(b)


_INS = ["x", "L0_conv_w_qkv", "L0_conv_w_dw", "L0_conv_w_pw", "L0_conv_w_proj", "L1_conv_W_theta",
        "L1_conv_b_theta", "L1_conv_W_phi", "L1_conv_b_phi", "L1_conv_W_fuse", "L1_conv_b_fuse"]


def kernel(**inputs):
    import concourse.bacc as bacc
    from concourse.bass_utils import run_bass_kernel_spmd

    nc = bacc.Bacc("TRN2", target_bir_lowering=False, num_devices=1)
    arrays = {n: np.ascontiguousarray(inputs[n]) for n in _INS}
    arrays["identity"] = np.eye(P, dtype=np.float32)
    arrays["shape_constants"] = shape_constants()
    args, in_map = [], {}
    for name, a in arrays.items():
        in_map[f"in_{name}"] = a
        args.append(nc.dram_tensor(f"in_{name}", a.shape, mybir.dt.from_np(a.dtype), kind="ExternalInput").ap())
    out = nc.dram_tensor("out_0", (B, C, H, W), F32, kind="ExternalOutput").ap()
    conv_attention_kernel(nc, *args, out)
    r = run_bass_kernel_spmd(nc, [in_map], core_ids=[0])
    return r.results[0]["out_0"]
```

```python
from contextlib import ExitStack

import numpy as np

import concourse.bass as bass
from concourse import mybir

F32 = mybir.dt.float32
ALU = mybir.AluOpType
ACT = mybir.ActivationFunctionType
AX_X = mybir.AxisListType.X

P = 128
B, C, H, W = 4, 128, 16, 16
N = H * W
E = 8
HEADS = 16
KINDS = 3
GROUPS = HEADS * KINDS
TAPS = 5
HP, WP = H // 2, W // 2
PR, PCOL = HP + 2, WP + 2
ROW = B * PCOL
PLANE = PR * ROW
WIN = 3
SLOT = HP * ROW
KROWS = WIN * 4 * E
NPIX = B * HP * WP
D = 64
EPS = 1e-15
WARM = 4
Q, K, V = 0, 1, 2
ORDER = (K, V, Q)
GPAD = (TAPS + 1) * TAPS + 2
GLEN = GPAD + GROUPS * TAPS * TAPS + 8


def shape_constants():
    p = np.arange(P)[:, None]
    m = np.arange(P)[None, :]
    same0 = p % HEADS == m % HEADS
    same1 = p // E == m // E
    cross = p // E == m % HEADS
    gather = p == m % 32 // E * 32 + m // 32 * E + m % E
    pick0 = (p % 32 < HEADS) & (p % HEADS == m % HEADS)
    pick1 = (p % 2 == 0) & (p % 32 // 2 == m // E)
    u, py, px = p // 32, p // 16 % 2, p // 8 % 2
    valid = []
    for v in range(WIN):
        for aa, bb in ((0, 0), (0, 1), (1, 0), (1, 1)):
            dy = 2 * u + py - (1 - aa)
            dx = 2 * v + px - (1 - bb)
            valid.append((dy >= 0) & (dy < TAPS) & (dx >= 0) & (dx < TAPS))
    total = (p % E == m[:, :32] % E) & (p // 32 == m[:, :32] // E)
    parts = [same0, same1, pick0, pick1, cross, gather, total, *valid]
    return np.concatenate([np.asarray(a, np.float32) for a in parts], axis=1)


def conv_attention_kernel(nc, x, w_qkv, w_dw, w_pw, w_proj, w_theta, b_theta, w_phi, b_phi,
                          w_fuse, b_fuse, const_in, out):
    with ExitStack() as ctx:
        def sb(name, *shape):
            return ctx.enter_context(nc.sbuf_tensor(name, list(shape), F32))

        def sem(name):
            return ctx.enter_context(nc.semaphore(name))

        xs = sb("xs", P, B, N)
        wqkv_n = sb("wqkv_n", P, KINDS, C)
        wpw_n = sb("wpw_n", P, KINDS, E)
        wproj_n = sb("wproj_n", P, 2 * P)
        wfuse_n = sb("wfuse_n", P, C)
        wth_n = sb("wth_n", D, C)
        wph_n = sb("wph_n", D, C)
        bth = sb("bth", D, 1)
        bph = sb("bph", D, 1)
        bfu = sb("bfu", P, 1)
        ident = sb("ident", P, P)
        consts = sb("consts", P, 6 * P + 32 + 4 * WIN)
        same = [consts[:, 0:P], consts[:, P:2 * P]]
        pick = consts[:, 2 * P:4 * P].rearrange("p (a m) -> p a m", a=2)
        pick_b = sb("pick_b", P, B, 2, P)
        cross, gather = consts[:, 4 * P:5 * P], consts[:, 5 * P:6 * P]
        total = consts[:, 6 * P:6 * P + 32]
        valid = consts[0:KROWS, 6 * P + 32:6 * P + 32 + 4 * WIN]
        warm = sb("warm", P, N)
        wqkv_t = sb("wqkv_t", P, KINDS, P)
        wpw_r = sb("wpw_r", P, KINDS, WIN * 4, E)
        wpw_t = sb("wpw_t", KROWS, GROUPS * E)
        wproj_t = sb("wproj_t", P, 2, P)
        wfuse_t = sb("wfuse_t", P, C)
        wth_t = sb("wth_t", P, D)
        wph_t = sb("wph_t", P, D)
        taps = sb("taps", KROWS, GLEN)
        wsel = sb("wsel", KROWS, GROUPS, 4 * WIN)
        wconv = sb("wconv", KROWS, KINDS, HEADS, 4 * WIN, E)
        planes = sb("planes", P, KINDS, 4, PLANE)
        slots = sb("slots", KROWS, KINDS, HEADS, SLOT)
        rq = [sb(f"rq{a}", P, B, N) for a in range(2)]
        kt0 = sb("kt0", P, B, 2, P)
        vt0 = sb("vt0", P, B, 2, P)
        conv = sb("conv", P, KINDS, 4, NPIX)
        kt1 = sb("kt1", P, 2, 4, P)
        vt1 = sb("vt1", P, 2, 4, P)
        vk = [sb(f"vk{a}", P, B, P) for a in range(2)]
        ks = [sb(f"ks{a}", P, B, 32) for a in range(2)]
        m2 = [sb(f"m2{a}", P, B, P) for a in range(2)]
        ksum0 = sb("ksum0", P, B)
        ksum1 = sb("ksum1", P, 4, B)
        relu_k = sb("relu_k", P, N)
        den = [sb(f"den{a}", P, N) for a in range(2)]
        rden = [sb(f"rden{a}", P, N) for a in range(2)]
        qs = [sb(f"qs{a}", P, B, N) for a in range(2)]
        x1 = sb("x1", P, B, N)
        theta = sb("theta", D, B, N)
        phi = sb("phi", D, B, N)
        gf = sb("gf", P, B, 2, C)
        mx = sb("mx", P, B, 2)
        nmx = sb("nmx", P, B, 2)
        rs = sb("rs", P, B, 2)
        rrs = sb("rrs", P, B, 2)
        spare = planes[:, :, :, :].rearrange("p k a l -> p (k a l)")
        pr = spare[:, 0:2 * B * N].rearrange("p (b q n) -> p b q n", b=B, q=2)
        pt = spare[:, 2 * B * N:4 * B * N].rearrange("p (b k n) -> p b k n", b=B, k=2)
        pn = conv[:, :, :, :].rearrange("p k r n -> p (k r n)")[:, 0:2 * B * N].rearrange(
            "p (b q n) -> p b q n", b=B, q=2)
        ys = kt0[:, :, :, :].rearrange("p b t c -> p b (t c)")

        bank = [ctx.enter_context(nc.psum_tensor(f"bank{i}", [P, 512], F32)) for i in range(8)]

        taps_d = nc.dram_tensor("taps_d", [E, GROUPS * TAPS * TAPS], F32, kind="Internal").ap()
        planes_d = [nc.dram_tensor(f"planes_d{k}", [4, P, PLANE], F32, kind="Internal").ap()
                    for k in range(KINDS)]

        ld_wqkv, ld_x, ld_const = sem("ld_wqkv"), sem("ld_x"), sem("ld_const")
        ld_wpw, ld_wproj, ld_wl1, ld_bias = sem("ld_wpw"), sem("ld_wproj"), sem("ld_wl1"), sem("ld_bias")
        taps_in_dram, ld_taps = sem("taps_in_dram"), sem("ld_taps")
        planes_in_dram = [sem(f"planes_in_dram{k}") for k in range(KINDS)]
        ld_slots = [sem(f"ld_slots{n}") for n in range(2 * KINDS)]
        stored = sem("stored")
        border_zero, taps_zero, warm_set, ident_set = sem("border_zero"), sem("taps_zero"), sem("warm_set"), sem("ident_set")
        pick_zero, pick_set = sem("pick_zero"), sem("pick_set")
        wconv_pool, wconv_dve, wsel_done = sem("wconv_pool"), sem("wconv_dve"), sem("wsel_done")
        wt_mm, wt_out = sem("wt_mm"), sem("wt_out")
        wpw_copied = sem("wpw_copied")
        wpw_mm, wpw_out = sem("wpw_mm"), sem("wpw_out")
        wpr_mm, wpr_out = sem("wpr_mm"), sem("wpr_out")
        wl1_mm, wl1_out = sem("wl1_mm"), sem("wl1_out")
        nat_mm, nat_act, nat_dve = sem("nat_mm"), sem("nat_act"), sem("nat_dve")
        rq0_act, rq0_dve = sem("rq0_act"), sem("rq0_dve")
        tok_mm, kt0_out, vt0_out = sem("tok_mm"), sem("kt0_out"), sem("vt0_out")
        vk_mm = [sem(f"vk_mm{a}") for a in range(2)]
        vk_out = [sem(f"vk_out{a}") for a in range(2)]
        den_mm = [sem(f"den_mm{a}") for a in range(2)]
        den_out = [sem(f"den_out{a}") for a in range(2)]
        rden_out = [sem(f"rden_out{a}") for a in range(2)]
        m2_mm = [sem(f"m2_mm{a}") for a in range(2)]
        m2_out = [sem(f"m2_out{a}") for a in range(2)]
        bc_mm = [sem(f"bc_mm{a}") for a in range(2)]
        qs_out = [sem(f"qs_out{a}") for a in range(2)]
        conv_mm, conv_act, conv_dve = sem("conv_mm"), sem("conv_act"), sem("conv_dve")
        tr_k_mm, tr_v_mm, kt1_out, vt1_out = sem("tr_k_mm"), sem("tr_v_mm"), sem("kt1_out"), sem("vt1_out")
        natq_mm, rq1_act, rq1_dve = sem("natq_mm"), sem("rq1_act"), sem("rq1_dve")
        proj_mm, x1_out = sem("proj_mm"), sem("x1_out")
        ks0_sum, ks1_sum, ks_out = sem("ks0_sum"), sem("ks1_sum"), [sem(f"ks_out{a}") for a in range(2)]
        tf_mm, tp_out, gf_out = sem("tf_mm"), sem("tp_out"), sem("gf_out")
        f_mm, mx_out, nmx_out, exp_out = sem("f_mm"), sem("mx_out"), sem("nmx_out"), sem("exp_out")
        rrs_out, pn_out = sem("rrs_out"), sem("pn_out")
        pt_mm, pt_out = sem("pt_mm"), sem("pt_out")
        y_mm, y_out = sem("y_mm"), sem("y_out")

        def parity(t, py, px, order="y b x"):
            v = t[:, :, :].rearrange(f"c b (y p x q) -> c p q {order}", p=2, q=2, y=HP, x=WP)
            return v[:, py, px]

        def split(i, order="y b x"):
            return bank[i][:, :].rearrange(f"c (q {order}) -> c q {order}", q=2, b=B, y=HP, x=WP)

        def conv_weights(kind, heads):
            sel = wsel[:, :, :].rearrange("p (h k) w -> p k h w", k=KINDS)[:, kind, heads]
            pw = wpw_t[:, :].rearrange("p (h k o) -> p k h o", k=KINDS, o=E)[:, kind, heads]
            shape = [KROWS, heads.stop - heads.start, 4 * WIN, E]
            return (wconv[:, kind, heads], sel.unsqueeze(3).broadcast_to(shape),
                    pw.unsqueeze(2).broadcast_to(shape))

        def plane_rows(kind, py):
            v = planes[:, kind, 2 * py:2 * py + 2, ROW:PLANE - ROW]
            return v.rearrange("c q (m x) -> c q m x", x=PCOL)[:, :, :, 1:1 + WP]

        def plane_bank(kind, py):
            return bank[NAT[kind][py]][:, :].rearrange("c (q m x) -> c q m x", q=2, x=WP)

        NAT = {K: (4, 5), V: (6, 7), Q: (0, 3)}
        CONV = {K: (0, 3), V: (2, 1), Q: (0, 3)}
        FIRST, SECOND = (2, 1, 0, 3), (4, 5, 6, 7)

        def conv_out(kind, half):
            return conv[:, kind, 2 * half:2 * half + 2, :].rearrange("p r n -> p (r n)")

        def tokens(t, pair):
            return t[:, 2 * pair:2 * pair + 2].rearrange("p b t c -> p (b t c)")

        def by_phase(t, pair):
            return t[:, pair].rearrange("p a (h e) -> p h a e", e=E)

        def tr_bank(i):
            return bank[i][:, :].rearrange("p (h a e) -> p h a e", a=4, e=E)

        block = ctx.enter_context(nc.Block())

        @block.sync
        def _(sp):
            sp.dma_start(wqkv_n[:, :, :], w_qkv.rearrange("(n p) c u v -> p n (c u v)", p=P)).then_inc(ld_wqkv, 16)
            sp.dma_start(wpw_n[:, :, :], w_pw.rearrange("(n p) c u v -> p n (c u v)", p=P)).then_inc(ld_wpw, 16)
            sp.wait_ge(taps_zero, 2)
            sp.wait_ge(taps_in_dram, 16)
            for s in range(WIN * 4):
                u, py, px = s // 4, s // 2 % 2, s % 2
                at = GPAD - TAPS * (2 * u + py) - px
                sp.dma_start(taps[E * s:E * (s + 1), at:at + GROUPS * TAPS * TAPS], taps_d).then_inc(ld_taps, 16)

            def planes_out(i):
                sp.wait_ge(nat_act, i + 1)
                sp.wait_ge(nat_dve, i + 1)
                sp.dma_start(planes_d[ORDER[i]].rearrange("a p l -> p a l"),
                             planes[:, ORDER[i], :, :]).then_inc(planes_in_dram[ORDER[i]], 16)

            def slots_in(i):
                kind = ORDER[i]
                sp.wait_ge(planes_in_dram[kind], 16)
                src = planes_d[kind].rearrange("a (c g) l -> (a c) g l", c=E)
                for half in range(2):
                    heads = slice(8 * half, 8 * (half + 1))
                    for u in range(WIN):
                        sp.dma_start(slots[32 * u:32 * (u + 1), kind, heads, :],
                                     src[:, heads, u * ROW:u * ROW + SLOT]).then_inc(ld_slots[2 * i + half], 16)

            sp.wait_ge(border_zero, 2)
            planes_out(0)
            planes_out(1)
            slots_in(0)
            planes_out(2)
            slots_in(1)
            slots_in(2)
            for b in range(B):
                sp.wait_ge(y_out, b + 1)
                sp.dma_start(out[b].rearrange("c h w -> c (h w)"), ys[:, b, :]).then_inc(stored, 16)
            sp.wait_ge(stored, 16 * B)

        @block.gpsimd
        def _(pool):
            nc.gpsimd.memset(ident[:, :], 0.0).then_inc(ident_set, 1)
            pool.wait_ge(ident_set, 1)
            nc.gpsimd.affine_select(out=ident[:, :], in_=ident[:, :], compare_op=ALU.not_equal, fill=1.0,
                                    base=0, pattern=[[-1, P]], channel_multiplier=1).then_inc(ident_set, 1)
            nc.gpsimd.memset(taps[:, 0:GPAD], 0.0).then_inc(taps_zero, 1)
            nc.gpsimd.memset(taps[:, GLEN - 40:GLEN], 0.0).then_inc(taps_zero, 1)
            pool.dma_start(consts[:, :], const_in).then_inc(ld_const, 16)
            allp = planes[:, :, :, :].rearrange("c k a l -> c (k a) l")
            rows = allp.rearrange("c a (r l) -> c a r l", r=PR)
            nc.gpsimd.memset(rows[:, :, 0:PR:PR - 1, :], 0.0).then_inc(border_zero, 1)
            cols = allp[:, :, ROW:PLANE - ROW].rearrange("c a (m x) -> c a m x", x=PCOL)
            nc.gpsimd.memset(cols[:, :, :, 0:PCOL:PCOL - 1], 0.0).then_inc(border_zero, 1)
            pool.dma_start(wproj_n[:, :], w_proj.rearrange("o c u v -> o (c u v)")).then_inc(ld_wproj, 16)
            pool.dma_start(wfuse_n[:, :], w_fuse).then_inc(ld_wl1, 16)
            pool.dma_start(wth_n[:, :], w_theta).then_inc(ld_wl1, 16)
            pool.dma_start(wph_n[:, :], w_phi).then_inc(ld_wl1, 16)
            pool.dma_start(bth[:, :], b_theta.rearrange("(p o) -> p o", o=1)).then_inc(ld_bias, 16)
            pool.dma_start(bph[:, :], b_phi.rearrange("(p o) -> p o", o=1)).then_inc(ld_bias, 16)
            pool.dma_start(bfu[:, :], b_fuse.rearrange("(p o) -> p o", o=1)).then_inc(ld_bias, 16)
            nc.gpsimd.memset(pick_b[:, :, :, :], 0.0).then_inc(pick_zero, 1)
            pool.wait_ge(ld_const, 16)
            pool.wait_ge(pick_zero, 1)
            for b in range(B):
                rows = slice(32 * b, 32 * (b + 1))
                if b:
                    pool.wait_ge(pick_set, b)
                nc.gpsimd.tensor_copy(pick_b[rows, b], pick[rows]).then_inc(pick_set, 1)
            pool.wait_ge(pick_set, B)
            pool.wait_ge(wsel_done, 2)
            pool.wait_ge(wpw_out, 1)
            for kind in (V, Q):
                nc.gpsimd.tensor_tensor(*conv_weights(kind, slice(0, HEADS)), ALU.mult).then_inc(wconv_pool, 1)

        @block.scalar
        def _(act):
            act.dma_start(xs[:, :, :], x.rearrange("b c h w -> c b (h w)")).then_inc(ld_x, 16)
            act.dma_start(taps_d.rearrange("c (g t) -> g c t", t=TAPS * TAPS),
                          w_dw.rearrange("(g c) o u v -> g c (o u v)", c=E)).then_inc(taps_in_dram, 16)
            act.wait_ge(ld_wpw, 16)
            nc.scalar.activation(wpw_r[:, :, :, :], wpw_n[:, :, :].unsqueeze(2).broadcast_to([P, KINDS, WIN * 4, E]),
                                 ACT.Copy).then_inc(wpw_copied, 1)
            for i, kind in enumerate(ORDER):
                act.wait_ge(nat_mm, 2 * i + 1)
                nc.scalar.activation(plane_rows(kind, 0), plane_bank(kind, 0), ACT.Copy).then_inc(nat_act, 1)
            for px in range(2):
                nc.scalar.activation(parity(rq[0], 0, px), split(NAT[Q][0])[:, px], ACT.Relu).then_inc(rq0_act, 1)
            for pair in range(2):
                act.wait_ge(tok_mm, 2 * pair + 1)
                nc.scalar.activation(tokens(kt0, pair), bank[4 + 2 * pair][:, :], ACT.Relu).then_inc(kt0_out, 1)
                if pair == 0:
                    act.wait_ge(nat_act, 1)
                    act.wait_ge(nat_dve, 1)
                for b in range(2 * pair, 2 * pair + 2):
                    src = planes[:, K, :, ROW:PLANE - ROW].rearrange("c a (y b x) -> c b a y x", b=B, x=PCOL)
                    if b:
                        act.wait_ge(ks0_sum, b)
                    nc.scalar.activation(relu_k[:, :].rearrange("c (a y x) -> c a y x", a=4, y=HP),
                                         src[:, b, :, :, 1:1 + WP], ACT.Relu,
                                         accum_out=ksum0[:, b:b + 1]).then_inc(ks0_sum, 1)
            act.wait_ge(m2_mm[0], 1)
            nc.scalar.activation(m2[0][:, :, :].rearrange("p b c -> p (b c)"), bank[7][:, :], ACT.Copy).then_inc(m2_out[0], 1)
            for i, kind in enumerate(ORDER):
                act.wait_ge(conv_mm, 2 * i + 1)
                nc.scalar.activation(conv_out(kind, 0), bank[CONV[kind][0]][:, :],
                                     ACT.Relu if kind == K else ACT.Copy).then_inc(conv_act, 1)
                if kind == V:
                    for pair in range(2):
                        act.wait_ge(tr_k_mm, pair + 1)
                        nc.scalar.activation(by_phase(kt1, pair), tr_bank(6 + pair), ACT.Copy).then_inc(kt1_out, 1)
            act.wait_ge(natq_mm, 1)
            for bb in range(2):
                nc.scalar.activation(parity(rq[1], 1, 1 - bb, "b y x"), split(2, "b y x")[:, bb], ACT.Relu).then_inc(rq1_act, 1)
            act.wait_ge(m2_mm[1], 1)
            nc.scalar.activation(m2[1][:, :, :].rearrange("p b c -> p (b c)"), bank[5][:, :], ACT.Copy).then_inc(m2_out[1], 1)
            act.wait_ge(ld_bias, 48)

            def theta_phi(b):
                act.wait_ge(tf_mm, b + 1)
                src = bank[SECOND[b]]
                nc.scalar.activation(theta[:, b, :], src[0:D, 0:N], ACT.Identity, bias=bth[:, 0:1]).then_inc(tp_out, 1)
                nc.scalar.activation(phi[:, b, :], src[D:2 * D, 0:N], ACT.Identity, bias=bph[:, 0:1]).then_inc(tp_out, 1)

            def values(b):
                nc.scalar.activation(gf[:, b].rearrange("p k c -> p (k c)"), bank[SECOND[b]][:, N:2 * N],
                                     ACT.Copy).then_inc(gf_out, 1)

            def exponentials(b):
                act.wait_ge(nmx_out, b + 1)
                for qc in range(2):
                    nc.scalar.activation(pr[:, b, qc, :], bank[FIRST[b]][:, qc * N:(qc + 1) * N], ACT.Exp,
                                         bias=nmx[:, b, qc:qc + 1], scale=D ** -0.5,
                                         accum_out=rs[:, b, qc:qc + 1]).then_inc(exp_out, 1)

            for step, b in ((theta_phi, 0), (values, 0), (theta_phi, 1), (values, 1), (theta_phi, 2), (exponentials, 0),
                            (values, 2), (theta_phi, 3), (exponentials, 1), (values, 3), (exponentials, 2), (exponentials, 3)):
                step(b)

        @block.vector
        def _(dve):
            nc.vector.memset(warm[:, :], 0.0).then_inc(warm_set, 1)
            dve.wait_ge(wt_mm, 1)
            src = bank[0][:, 0:KINDS * P].rearrange("c (h k e) -> c k e h", k=KINDS, e=E)
            for kind in ORDER:
                nc.vector.tensor_copy(wqkv_t[:, kind].rearrange("c (e h) -> c e h", e=E), src[:, kind]).then_inc(wt_out, 1)
            for i, kind in enumerate(ORDER):
                dve.wait_ge(nat_mm, 2 * i + 2)
                nc.vector.tensor_copy(plane_rows(kind, 1), plane_bank(kind, 1)).then_inc(nat_dve, 1)
                if i == 1:
                    dve.wait_ge(wpw_mm, 1)
                    nc.vector.tensor_copy(wpw_t[:, :], bank[1][0:KROWS, 0:GROUPS * E]).then_inc(wpw_out, 1)
            for px in range(2):
                nc.vector.tensor_scalar_max(parity(rq[0], 1, px), split(NAT[Q][1])[:, px], 0.0).then_inc(rq0_dve, 1)

            def v_by_token(pair):
                dve.wait_ge(tok_mm, 2 * pair + 2)
                nc.vector.tensor_copy(tokens(vt0, pair), bank[5 + 2 * pair][:, :]).then_inc(vt0_out, 1)

            v_by_token(0)
            dve.wait_ge(ld_taps, 16 * WIN * 4)
            dve.wait_ge(ld_const, 16)
            for aa in range(2):
                at = GPAD + TAPS * (aa - 1) - 1
                src = taps[:, at:at + GROUPS * TAPS * TAPS].rearrange("p (g t) -> p g t", t=TAPS * TAPS)[:, :, 0:2 * WIN]
                src = src.rearrange("p g (v b) -> p g v b", b=2)
                m = valid.rearrange("p (v a b) -> p a v b", a=2, b=2)[:, aa].unsqueeze(1).broadcast_to([KROWS, GROUPS, WIN, 2])
                dst = wsel[:, :, :].rearrange("p g (v a b) -> p a g v b", a=2, b=2)[:, aa]
                nc.vector.tensor_tensor(dst, src, m, ALU.mult).then_inc(wsel_done, 1)
            v_by_token(1)
            dve.wait_ge(wsel_done, 2)
            dve.wait_ge(wpw_out, 1)
            nc.vector.tensor_tensor(*conv_weights(K, slice(0, 8)), ALU.mult).then_inc(wconv_dve, 1)
            dve.wait_ge(wpr_mm, 1)
            nc.vector.tensor_copy(wproj_t[:, :, :].rearrange("p a c -> p (a c)"), bank[2][:, 0:2 * P]).then_inc(wpr_out, 1)

            def attend_sums(a, banks):
                for pair in range(2):
                    images = slice(2 * pair, 2 * pair + 2) if a == 0 else slice(pair, B, 2)
                    dve.wait_ge(vk_mm[a], pair + 1)
                    src = bank[banks[pair]][:, :].rearrange("p (b n) -> p b n", b=2)
                    mask = (cross, same[1])[a].unsqueeze(1).broadcast_to([P, 2, P])
                    nc.vector.tensor_tensor(vk[a][:, images, :], src[:, :, 0:P], mask, ALU.mult).then_inc(vk_out[a], 1)

            def key_sums(a, sums):
                shape = [P, B, 2, HEADS] if a == 0 else [P, B, HEADS, 2]
                if a == 0:
                    mask = same[0][:, 0:32].rearrange("p (t h) -> p t h", t=2)
                    dst = ks[0][:, :, :].rearrange("p b (t h) -> p b t h", t=2)
                else:
                    mask = same[1].rearrange("p (h e) -> p h e", e=E)[:, :, 0:2]
                    dst = ks[1][:, :, :].rearrange("p b (h t) -> p b h t", t=2)
                nc.vector.tensor_tensor(dst, sums.unsqueeze(2).unsqueeze(3).broadcast_to(shape),
                                        mask.unsqueeze(1).broadcast_to(shape), ALU.mult).then_inc(ks_out[a], 1)

            def reciprocals(a, i):
                dve.wait_ge(den_mm[a], 1)
                nc.vector.tensor_scalar_add(den[a][:, :], bank[i][:, 0:N], EPS).then_inc(den_out[a], 1)
                dve.wait_ge(den_out[a], 1)
                nc.vector.reciprocal(rden[a][:, :], den[a][:, :]).then_inc(rden_out[a], 1)

            def scale_q(a, banks):
                for pair in range(2):
                    dve.wait_ge(bc_mm[a], pair + 1)
                    o = qs[a][:, 2 * pair:2 * pair + 2, :].rearrange("p b n -> p (b n)")
                    q = rq[a][:, 2 * pair:2 * pair + 2, :].rearrange("p b n -> p (b n)")
                    nc.vector.tensor_tensor(o, bank[banks[pair]][:, :], q, ALU.mult).then_inc(qs_out[a], 1)

            dve.wait_ge(ks0_sum, B)
            key_sums(0, ksum0[:, :])
            attend_sums(0, (4, 5))
            reciprocals(0, 6)
            nc.vector.tensor_tensor(*conv_weights(K, slice(8, HEADS)), ALU.mult).then_inc(wconv_dve, 1)
            dve.wait_ge(wl1_mm, 1)
            nc.vector.tensor_copy(wfuse_t[:, :], bank[1][:, 0:C]).then_inc(wl1_out, 1)
            nc.vector.tensor_copy(wth_t[:, :], bank[1][:, C:C + D]).then_inc(wl1_out, 1)
            nc.vector.tensor_copy(wph_t[:, :], bank[1][:, C + D:C + 2 * D]).then_inc(wl1_out, 1)
            for i, kind in enumerate(ORDER):
                if kind == V:
                    scale_q(0, (4, 5))
                dve.wait_ge(conv_mm, 2 * i + 2)
                if kind == K:
                    nc.vector.tensor_scalar_max(conv_out(kind, 1), bank[CONV[kind][1]][:, :], 0.0).then_inc(conv_dve, 1)
                    for half in range(2):
                        dve.wait_ge((conv_act, conv_dve)[half], 1)
                        src = conv[:, K, 2 * half:2 * half + 2, :].rearrange("p r (b n) -> p r b n", b=B)
                        nc.vector.tensor_reduce(ksum1[:, 2 * half:2 * half + 2, :], src, AX_X, ALU.add).then_inc(ks1_sum, 1)
                else:
                    nc.vector.tensor_copy(conv_out(kind, 1), bank[CONV[kind][1]][:, :]).then_inc(conv_dve, 1)
                if kind == V:
                    for pair in range(2):
                        dve.wait_ge(tr_v_mm, pair + 1)
                        nc.vector.tensor_copy(by_phase(vt1, pair), tr_bank(4 + pair)).then_inc(vt1_out, 1)
            dve.wait_ge(vk_mm[1], 1)
            key_sums(1, bank[6][:, 2 * N - B:2 * N])
            attend_sums(1, (6, 7))
            dve.wait_ge(natq_mm, 2)
            for bb in range(2):
                nc.vector.tensor_scalar_max(parity(rq[1], 0, 1 - bb, "b y x"), split(1, "b y x")[:, bb], 0.0).then_inc(rq1_dve, 1)
            reciprocals(1, 4)
            scale_q(1, (6, 7))

            def first_layer(b):
                dve.wait_ge(proj_mm, b + 1)
                nc.vector.tensor_tensor(x1[:, b, :], bank[FIRST[b]][:, 0:N], xs[:, b, :], ALU.add).then_inc(x1_out, 1)

            def maxima(b):
                dve.wait_ge(f_mm, b + 1)
                nc.vector.tensor_reduce(mx[:, b, :], bank[FIRST[b]][:, :].rearrange("p (q n) -> p q n", q=2),
                                        AX_X, ALU.max).then_inc(mx_out, 1)
                dve.wait_ge(mx_out, b + 1)
                nc.vector.tensor_scalar_mul(nmx[:, b, :], mx[:, b, :], -D ** -0.5).then_inc(nmx_out, 1)

            def normalize(b):
                dve.wait_ge(exp_out, 2 * b + 2)
                nc.vector.reciprocal(rrs[:, b, :], rs[:, b, :]).then_inc(rrs_out, 1)
                dve.wait_ge(rrs_out, b + 1)
                for qc in range(2):
                    nc.vector.tensor_scalar_mul(pn[:, b, qc, :], pr[:, b, qc, :], rrs[:, b, qc:qc + 1]).then_inc(pn_out, 1)

            def transposed(b):
                dve.wait_ge(pt_mm, b + 1)
                nc.vector.tensor_copy(pt[:, b].rearrange("p k n -> p (k n)"), bank[SECOND[b]][:, :]).then_inc(pt_out, 1)

            def result(b):
                dve.wait_ge(y_mm, b + 1)
                nc.vector.scalar_tensor_tensor(ys[:, b, :], bank[FIRST[b]][:, 0:N], bfu[:, 0:1], x1[:, b, :],
                                               ALU.add, ALU.add).then_inc(y_out, 1)

            dve.wait_ge(ld_bias, 48)
            for step, b in ((first_layer, 0), (first_layer, 1), (first_layer, 2), (first_layer, 3), (maxima, 0),
                            (maxima, 1), (normalize, 0), (maxima, 2), (transposed, 0), (normalize, 1), (maxima, 3),
                            (transposed, 1), (normalize, 2), (result, 0), (transposed, 2), (normalize, 3),
                            (result, 1), (transposed, 3), (result, 2), (result, 3)):
                step(b)

        @block.tensor
        def _(pe):
            pe.wait_ge(warm_set, 1)
            for _ in range(WARM):
                nc.tensor.matmul(bank[3][:, 0:N], warm[:, 0:P], warm[:, :], start=True, stop=True)
            pe.wait_ge(ld_wqkv, 16)
            pe.wait_ge(ident_set, 2)
            for n in range(KINDS):
                last = nc.tensor.transpose(bank[0][:, n * P:(n + 1) * P], wqkv_n[:, n, :], ident[:, :])
            last.then_inc(wt_mm, 1)
            pe.wait_ge(ld_x, 16)

            def natural(i):
                kind = ORDER[i]
                pe.wait_ge(wt_out, i + 1 if kind != Q else KINDS)
                for py in range(2):
                    for px in range(2):
                        last = nc.tensor.matmul(bank[NAT[kind][py]][:, px * NPIX:(px + 1) * NPIX],
                                                wqkv_t[:, kind, :], parity(xs, py, px), start=True, stop=True)
                    last.then_inc(nat_mm, 1)

            natural(0)
            natural(1)
            pe.wait_ge(wpw_copied, 1)
            for n in range(KINDS):
                src = wpw_r[:, n].rearrange("p s e -> p (s e)")
                last = nc.tensor.transpose(bank[1][0:KROWS, n * P:(n + 1) * P], src, ident[:, :])
            last.then_inc(wpw_mm, 1)
            natural(2)
            for pair in range(2):
                for kind, free in ((K, nat_act), (V, nat_dve)):
                    pe.wait_ge(free, pair + 1)
                    dst = bank[(4 if kind == K else 5) + 2 * pair]
                    w = wqkv_t[:, kind, :]
                    if kind == V:
                        w = w.rearrange("c (e h) -> c h e", e=E)
                    for n in range(4):
                        b, t = 2 * pair + n // 2, n % 2
                        last = nc.tensor.matmul(dst[:, n * P:(n + 1) * P], xs[:, b, t * P:(t + 1) * P],
                                                w, start=True, stop=True)
                    last.then_inc(tok_mm, 1)
            pe.wait_ge(ld_wproj, 16)
            nc.tensor.transpose(bank[2][:, 0:P], wproj_n[:, 0:P], ident[:, :])
            nc.tensor.transpose(bank[2][:, P:2 * P], wproj_n[:, P:2 * P], ident[:, :]).then_inc(wpr_mm, 1)
            pe.wait_ge(ld_wl1, 48)
            pe.wait_ge(wpw_out, 1)
            nc.tensor.transpose(bank[1][:, 0:C], wfuse_n[:, :], ident[:, :])
            nc.tensor.transpose(bank[1][:, C:C + D], wth_n[:, :], ident[0:D, 0:D])
            nc.tensor.transpose(bank[1][:, C + D:C + 2 * D], wph_n[:, :], ident[0:D, 0:D]).then_inc(wl1_mm, 1)
            pe.wait_ge(kt0_out, 1)
            pe.wait_ge(vt0_out, 1)
            for pair in range(2):
                pe.wait_ge(kt0_out, pair + 1)
                pe.wait_ge(vt0_out, pair + 1)
                for s in range(2):
                    b, at = 2 * pair + s, 256 * s
                    for t in range(2):
                        last = nc.tensor.matmul(bank[4 + pair][:, at:at + P], vt0[:, b, t, :], kt0[:, b, t, :],
                                                start=t == 0, stop=t == 1)
                last.then_inc(vk_mm[0], 1)

            def denominators(a, i):
                pe.wait_ge(ks_out[a], 1)
                for b in range(B):
                    last = nc.tensor.matmul(bank[i][32 * b:32 * (b + 1), 0:N], ks[a][:, b, :], rq[a][:, b, :],
                                            start=True, stop=True)
                last.then_inc(den_mm[a], 1)

            def projected_sums(a, i):
                pe.wait_ge(vk_out[a], 2)
                for b in range(B):
                    last = nc.tensor.matmul(bank[i][:, b * P:(b + 1) * P], vk[a][:, b, :], wproj_t[:, a, :],
                                            start=True, stop=True)
                last.then_inc(m2_mm[a], 1)

            def spread(a, pair, i):
                pe.wait_ge(rden_out[a], 1)
                pe.wait_ge(pick_set, B)
                for s in range(2):
                    b = 2 * pair + s
                    last = nc.tensor.matmul(bank[i][:, s * N:(s + 1) * N], pick_b[:, b, a, :], rden[a][:, :],
                                            start=True, stop=True)
                last.then_inc(bc_mm[a], 1)

            pe.wait_ge(rq0_act, 2)
            pe.wait_ge(rq0_dve, 2)
            pe.wait_ge(kt0_out, 2)
            denominators(0, 6)
            pe.wait_ge(wpr_out, 1)
            pe.wait_ge(vt0_out, 2)
            projected_sums(0, 7)

            def convolve(i, half):
                kind = ORDER[i]
                pe.wait_ge(ld_slots[2 * i + half], 16 * WIN)
                dst = bank[CONV[kind][half]]
                for r in (2 * half, 2 * half + 1):
                    at = (r - 2 * half) * NPIX
                    for v in range(WIN):
                        for j in range(4):
                            h = 4 * r + j
                            w = wconv[:, kind, h, 4 * v:4 * (v + 1), :].rearrange("p a o -> p (a o)")
                            src = slots[:, kind, h, :].rearrange("p (y b x) -> p b y x", b=B, x=PCOL)[:, :, :, v:v + WP]
                            last = nc.tensor.matmul(dst[32 * j:32 * (j + 1), at:at + NPIX], w, src,
                                                    start=v == 0, stop=v == WIN - 1)
                last.then_inc(conv_mm, 1)

            def by_token(kind, pair, i, done):
                for r in range(4):
                    src = conv[:, kind, r, pair * P:(pair + 1) * P]
                    last = nc.tensor.transpose(bank[i][:, r * P:(r + 1) * P], src, ident[:, :])
                last.then_inc(done, 1)

            pe.wait_ge(wconv_dve, 1)
            convolve(0, 0)
            pe.wait_ge(vk_out[0], 2)
            spread(0, 0, 4)
            spread(0, 1, 5)
            pe.wait_ge(wconv_dve, 2)
            convolve(0, 1)
            pe.wait_ge(wconv_pool, 1)
            convolve(1, 0)
            pe.wait_ge(conv_act, 1)
            pe.wait_ge(conv_dve, 1)
            pe.wait_ge(den_out[0], 1)
            by_token(K, 0, 6, tr_k_mm)
            pe.wait_ge(m2_out[0], 1)
            by_token(K, 1, 7, tr_k_mm)
            pe.wait_ge(wl1_out, 3)
            convolve(1, 1)
            pe.wait_ge(wconv_pool, 2)
            convolve(2, 0)
            pe.wait_ge(conv_act, 2)
            pe.wait_ge(conv_dve, 2)
            pe.wait_ge(qs_out[0], 2)
            by_token(V, 0, 4, tr_v_mm)
            by_token(V, 1, 5, tr_v_mm)
            convolve(2, 1)
            pe.wait_ge(kt1_out, 2)
            pe.wait_ge(ks1_sum, 2)
            for r in range(4):
                nc.tensor.matmul(bank[6][32 * r:32 * (r + 1), 2 * N - B:2 * N], total, ksum1[:, r, :], start=True, stop=True)
            pe.wait_ge(vt1_out, 2)
            for s in range(2):
                for pair in range(2):
                    at, rows = 256 * pair, slice(D * s, D * (s + 1))
                    for ph in range(4):
                        last = nc.tensor.matmul(bank[6 + s][:, at:at + P], vt1[rows, pair, ph, :], kt1[rows, pair, ph, :],
                                                start=ph == 0, stop=ph == 3)
                last.then_inc(vk_mm[1], 1)
            pe.wait_ge(conv_act, 3)
            pe.wait_ge(conv_dve, 3)
            for aa in range(2):
                for bb in range(2):
                    w = gather[:, 32 * (2 * aa + bb):32 * (2 * aa + bb + 1)]
                    for r in range(4):
                        last = nc.tensor.matmul(bank[2 - aa][32 * r:32 * (r + 1), bb * NPIX:(bb + 1) * NPIX], w,
                                                conv[:, Q, r, :], start=True, stop=True)
                last.then_inc(natq_mm, 1)
            pe.wait_ge(vt1_out, 2)
            projected_sums(1, 5)
            pe.wait_ge(rq1_act, 2)
            pe.wait_ge(rq1_dve, 2)
            denominators(1, 4)

            def project(b, a):
                if a == 1:
                    pe.wait_ge(m2_out[1], 1)
                    pe.wait_ge(qs_out[1], b // 2 + 1)
                last = nc.tensor.matmul(bank[FIRST[b]][:, 0:N], m2[a][:, b, :], qs[a][:, b, :],
                                        start=a == 0, stop=a == 1)
                if a == 1:
                    last.then_inc(proj_mm, 1)

            def theta_phi_values(b):
                pe.wait_ge(x1_out, b + 1)
                pe.wait_ge((den_out[1], m2_out[1], qs_out[1], qs_out[1])[b], (1, 1, 1, 2)[b])
                dst = bank[SECOND[b]]
                nc.tensor.matmul(dst[0:D, 0:N], wth_t[:, :], x1[:, b, :], start=True, stop=True)
                nc.tensor.matmul(dst[D:2 * D, 0:N], wph_t[:, :], x1[:, b, :], start=True, stop=True)
                for kc in range(2):
                    last = nc.tensor.matmul(dst[:, N + kc * C:N + (kc + 1) * C], x1[:, b, kc * P:(kc + 1) * P],
                                            wfuse_t[:, :], start=True, stop=True)
                last.then_inc(tf_mm, 1)

            def scores(b):
                pe.wait_ge(tp_out, 2 * b + 2)
                for qc in range(2):
                    last = nc.tensor.matmul(bank[FIRST[b]][:, qc * N:(qc + 1) * N], theta[:, b, qc * P:(qc + 1) * P],
                                            phi[:, b, :], start=True, stop=True)
                last.then_inc(f_mm, 1)

            def transpose_probs(b):
                pe.wait_ge(pn_out, 2 * b + 2)
                pe.wait_ge(gf_out, b + 1)
                for kc in range(2):
                    for qc in range(2):
                        at = kc * N + qc * P
                        last = nc.tensor.transpose(bank[SECOND[b]][:, at:at + P], pn[:, b, qc, kc * P:(kc + 1) * P], ident[:, :])
                last.then_inc(pt_mm, 1)

            def attend(b):
                pe.wait_ge(pt_out, b + 1)
                for kc in range(2):
                    last = nc.tensor.matmul(bank[FIRST[b]][:, 0:N], gf[:, b, kc, :], pt[:, b, kc, :],
                                            start=kc == 0, stop=kc == 1)
                last.then_inc(y_mm, 1)

            for b in range(B):
                project(b, 0)
            spread(1, 0, 6)
            spread(1, 1, 7)
            for b in range(B):
                project(b, 1)
            for step, b in ((theta_phi_values, 0), (theta_phi_values, 1), (theta_phi_values, 2), (scores, 0),
                            (theta_phi_values, 3), (scores, 1), (scores, 2), (transpose_probs, 0), (scores, 3),
                            (transpose_probs, 1), (attend, 0), (transpose_probs, 2), (attend, 1),
                            (transpose_probs, 3), (attend, 2), (attend, 3)):
                step(b)


_INS = ["x", "L0_conv_w_qkv", "L0_conv_w_dw", "L0_conv_w_pw", "L0_conv_w_proj", "L1_conv_W_theta",
        "L1_conv_b_theta", "L1_conv_W_phi", "L1_conv_b_phi", "L1_conv_W_fuse", "L1_conv_b_fuse"]


def kernel(**inputs):
    import concourse.bacc as bacc
    from concourse.bass_utils import run_bass_kernel_spmd

    nc = bacc.Bacc("TRN2", target_bir_lowering=False, num_devices=1)
    arrays = {n: np.ascontiguousarray(inputs[n]) for n in _INS}
    arrays["shape_constants"] = shape_constants()
    args, in_map = [], {}
    for name, a in arrays.items():
        in_map[f"in_{name}"] = a
        args.append(nc.dram_tensor(f"in_{name}", a.shape, mybir.dt.from_np(a.dtype), kind="ExternalInput").ap())
    out = nc.dram_tensor("out_0", (B, C, H, W), F32, kind="ExternalOutput").ap()
    conv_attention_kernel(nc, *args, out)
    r = run_bass_kernel_spmd(nc, [in_map], core_ids=[0])
    return r.results[0]["out_0"]
```

```python
from contextlib import ExitStack

import numpy as np

import concourse.bass as bass
from concourse import mybir

F32 = mybir.dt.float32
F32R = mybir.dt.float32r
ALU = mybir.AluOpType
ACT = mybir.ActivationFunctionType
AX_X = mybir.AxisListType.X

P = 128
B, C, H, W = 4, 128, 16, 16
N = H * W
E = 8
HEADS = 16
KINDS = 3
GROUPS = HEADS * KINDS
TAPS = 5
HP, WP = H // 2, W // 2
PR, PCOL = HP + 2, WP + 2
ROW = B * PCOL
PLANE = PR * ROW
WIN = 3
SLOT = HP * ROW
KROWS = WIN * 4 * E
NPIX = B * HP * WP
D = 64
EPS = 1e-15
Q, K, V = 0, 1, 2
ORDER = (K, Q, V)
CHUNKS = {K: (0, 1, 2, 3, 4), Q: (0, 2, 4), V: (0, 4)}
TLEN = GROUPS * TAPS * TAPS
TPAD = TAPS + 1
TSPAN = TPAD + TLEN
TROW = TSPAN + TAPS * TAPS
TFILL = -(-2 * E * TROW // P)


def shape_constants():
    p = np.arange(P)[:, None]
    m = np.arange(P)[None, :]
    same0 = p % HEADS == m % HEADS
    same1 = p // E == m // E
    cross = p // E == m % HEADS
    gather = p == m % 32 // E * 32 + m // 32 * E + m % E
    pick0 = (p % 32 < HEADS) & (p % HEADS == m % HEADS)
    pick1 = (p % 2 == 0) & (p % 32 // 2 == m // E)
    u, py, px = p // 32, p // 16 % 2, p // 8 % 2
    valid = []
    for v in range(WIN):
        for aa, bb in ((0, 0), (0, 1), (1, 0), (1, 1)):
            dy = 2 * u + py - (1 - aa)
            dx = 2 * v + px - (1 - bb)
            valid.append((dy >= 0) & (dy < TAPS) & (dx >= 0) & (dx < TAPS))
    total = (p % E == m[:, :32] % E) & (p // 32 == m[:, :32] // E)
    parts = [same0, same1, pick0, pick1, cross, gather, total, *valid]
    return np.concatenate([np.asarray(a, np.float32) for a in parts], axis=1)


def conv_attention_kernel(nc, x, w_qkv, w_dw, w_pw, w_proj, w_theta, b_theta, w_phi, b_phi,
                          w_fuse, b_fuse, const_in, out):
    with ExitStack() as ctx:
        def sb(name, *shape, dtype=F32):
            return ctx.enter_context(nc.sbuf_tensor(name, list(shape), dtype))

        def sem(name):
            return ctx.enter_context(nc.semaphore(name))

        xs = sb("xs", P, B, N)
        wqkv_n = sb("wqkv_n", P, KINDS, C)
        wpw_n = sb("wpw_n", P, KINDS, E)
        wproj_n = sb("wproj_n", P, 2 * P)
        wfuse_n = sb("wfuse_n", P, C)
        wth_n = sb("wth_n", D, C)
        wph_n = sb("wph_n", D, C)
        bth = sb("bth", D, 1)
        bph = sb("bph", D, 1)
        bfu = sb("bfu", P, 1)
        bth_s = sb("bth_s", D, 1)
        ident = sb("ident", P, P)
        consts = sb("consts", P, 6 * P + 32 + 4 * WIN)
        same = [consts[:, 0:P], consts[:, P:2 * P]]
        pick = consts[:, 2 * P:4 * P].rearrange("p (a m) -> p a m", a=2)
        pick_b = sb("pick_b", P, B, 2, P, dtype=F32R)
        cross, gather = consts[:, 4 * P:5 * P], consts[:, 5 * P:6 * P]
        total = consts[:, 6 * P:6 * P + 32]
        valid = consts[0:KROWS, 6 * P + 32:6 * P + 32 + 4 * WIN]
        warm = sb("warm", P, N)
        wqkv_t = sb("wqkv_t", P, KINDS, P)
        wpw_r = sb("wpw_r", P, KINDS, WIN * 4, E)
        wpw_t = sb("wpw_t", KROWS, GROUPS * E)
        wproj_t = sb("wproj_t", P, 2, P)
        wfuse_t = sb("wfuse_t", P, C)
        wtp_t = sb("wtp_t", P, 2 * D)
        taps = sb("taps", KROWS, TSPAN)
        wsel = sb("wsel", KROWS, GROUPS, 4 * WIN)
        wconv = sb("wconv", KROWS, KINDS, HEADS, 4 * WIN, E)
        planes = sb("planes", P, KINDS, 4, PLANE)
        slots = sb("slots", KROWS, KINDS, HEADS, SLOT)
        rq = [sb(f"rq{a}", P, B, N) for a in range(2)]
        kt0 = sb("kt0", P, B, 2, P)
        vt0 = sb("vt0", P, B, 2, P)
        conv = sb("conv", P, KINDS, 4, NPIX)
        kt1 = sb("kt1", P, 2, 4, P)
        vt1 = sb("vt1", P, 2, 4, P)
        vk = [sb(f"vk{a}", P, B, P) for a in range(2)]
        ks = [sb(f"ks{a}", P, B, 32) for a in range(2)]
        m2 = [sb(f"m2{a}", P, B, P) for a in range(2)]
        ksum0 = sb("ksum0", P, B)
        ksum1 = sb("ksum1", P, 4, B)
        k_copy = sb("k_copy", P, N)
        den = [sb(f"den{a}", P, N) for a in range(2)]
        rden = [sb(f"rden{a}", P, N) for a in range(2)]
        rden_hi = sb("rden_hi", P, N, dtype=F32R)
        rden_lo = sb("rden_lo", P, N, dtype=F32R)
        qs = [sb(f"qs{a}", P, B, N) for a in range(2)]
        x1 = sb("x1", P, B, N)
        theta = sb("theta", D, B, N)
        phi = sb("phi", D, B, N)
        gf = sb("gf", P, B, 2, C)
        nmx = sb("nmx", P, B, 2)
        rs = sb("rs", P, B, 2)
        rrs = sb("rrs", P, B, 2)
        kn, vn = qs[1], x1
        spare = planes[:, :, :, :].rearrange("p k a l -> p (k a l)")
        pr = spare[:, 0:2 * B * N].rearrange("p (b q n) -> p b q n", b=B, q=2)
        pt = spare[:, 2 * B * N:4 * B * N].rearrange("p (b k n) -> p b k n", b=B, k=2)
        pn = conv[:, :, :, :].rearrange("p k r n -> p (k r n)")[:, 0:2 * B * N].rearrange(
            "p (b q n) -> p b q n", b=B, q=2)
        ys = kt0[:, :, :, :].rearrange("p b t c -> p b (t c)")

        bank = [ctx.enter_context(nc.psum_tensor(f"bank{i}", [P, 512], F32)) for i in range(8)]

        taps_d = nc.dram_tensor("taps_d", [P * TFILL], F32, kind="Internal").ap()
        planes_d = {k: nc.dram_tensor(f"planes_d{k}", [4, P, PLANE], F32, kind="Internal").ap() for k in (K, Q)}

        ld_wqkv, ld_x, ld_const = sem("ld_wqkv"), sem("ld_x"), sem("ld_const")
        ld_wpw, ld_wproj, ld_wl1, ld_bias = sem("ld_wpw"), sem("ld_wproj"), sem("ld_wl1"), sem("ld_bias")
        taps_cleared, taps_in_dram, ld_taps = sem("taps_cleared"), sem("taps_in_dram"), sem("ld_taps")
        planes_in_dram = {k: sem(f"planes_in_dram{k}") for k in (K, Q)}
        ld_slots = {(k, r): sem(f"ld_slots{k}{r}") for k in ORDER for r in CHUNKS[k][:-1]}
        stored = sem("stored")
        border_zero, warm_set, ident_set = sem("border_zero"), sem("warm_set"), sem("ident_set")
        pick_zero, pick_set = sem("pick_zero"), sem("pick_set")
        wconv_pool, wconv_dve = sem("wconv_pool"), sem("wconv_dve")
        wsel_pool, wsel_dve = sem("wsel_pool"), sem("wsel_dve")
        wt_mm, wt_out = sem("wt_mm"), sem("wt_out")
        wpw_copied = sem("wpw_copied")
        wpw_mm, wpw_out = sem("wpw_mm"), sem("wpw_out")
        wpr_mm, wpr_out = sem("wpr_mm"), sem("wpr_out")
        wl1_mm, wl1_out = sem("wl1_mm"), sem("wl1_out")
        nat_mm, nat_act, nat_dve = sem("nat_mm"), sem("nat_act"), sem("nat_dve")
        rq0_act, rq0_dve = sem("rq0_act"), sem("rq0_dve")
        kn_act, kn_dve, vn_act, vn_dve = sem("kn_act"), sem("kn_dve"), sem("vn_act"), sem("vn_dve")
        kt0_mm, vt0_mm, kt0_out = sem("kt0_mm"), sem("vt0_mm"), sem("kt0_out")
        vt0_dve, vt0_act = sem("vt0_dve"), sem("vt0_act")
        vk_mm = [sem(f"vk_mm{a}") for a in range(2)]
        vk_out = [sem(f"vk_out{a}") for a in range(2)]
        den_mm = [sem(f"den_mm{a}") for a in range(2)]
        den_out = [sem(f"den_out{a}") for a in range(2)]
        rden_out = [sem(f"rden_out{a}") for a in range(2)]
        rden_split = [sem(f"rden_split{a}") for a in range(2)]
        m2_mm = [sem(f"m2_mm{a}") for a in range(2)]
        m2_out = [sem(f"m2_out{a}") for a in range(2)]
        m2_last_out = sem("m2_last_out")
        bc_mm = [sem(f"bc_mm{a}") for a in range(2)]
        qs_out = [sem(f"qs_out{a}") for a in range(2)]
        conv_mm, conv_act, conv_dve = sem("conv_mm"), sem("conv_act"), sem("conv_dve")
        tr_k_mm, tr_v_mm, kt1_out = sem("tr_k_mm"), sem("tr_v_mm"), sem("kt1_out")
        vt1_act, vt1_dve = sem("vt1_act"), sem("vt1_dve")
        natq_mm, rq1_act, rq1_dve = sem("natq_mm"), sem("rq1_act"), sem("rq1_dve")
        proj_mm, x1_out, tot_mm = sem("proj_mm"), sem("x1_out"), sem("tot_mm")
        ks0_sum, ks1_sum, ks_out = sem("ks0_sum"), sem("ks1_sum"), [sem(f"ks_out{a}") for a in range(2)]
        tf_mm, tp_out, gf_out = sem("tf_mm"), sem("tp_out"), [sem(f"gf_out{b}") for b in range(B)]
        bias_scaled, f_mm, nmx_out, exp_out = sem("bias_scaled"), sem("f_mm"), sem("nmx_out"), sem("exp_out")
        rrs_out, pn_out = sem("rrs_out"), sem("pn_out")
        pt_mm, pt_out = sem("pt_mm"), [sem(f"pt_out{b}") for b in range(B)]
        y_mm, y_out = sem("y_mm"), sem("y_out")

        def parity(t, py, px, order="y b x"):
            v = t[:, :, :].rearrange(f"c b (y p x q) -> c p q {order}", p=2, q=2, y=HP, x=WP)
            return v[:, py, px]

        def split(i, order="y b x"):
            return bank[i][:, :].rearrange(f"c (q {order}) -> c q {order}", q=2, b=B, y=HP, x=WP)

        def conv_weights(kind, heads):
            sel = wsel[:, :, :].rearrange("p (h k) w -> p k h w", k=KINDS)[:, kind, heads]
            pw = wpw_t[:, :].rearrange("p (h k o) -> p k h o", k=KINDS, o=E)[:, kind, heads]
            shape = [KROWS, heads.stop - heads.start, 4 * WIN, E]
            return (wconv[:, kind, heads], sel.unsqueeze(3).broadcast_to(shape),
                    pw.unsqueeze(2).broadcast_to(shape))

        def selected_taps(aa):
            src = taps[:, TAPS * aa:TAPS * aa + TLEN].rearrange("p (g t) -> p g t", t=TAPS * TAPS)[:, :, 0:2 * WIN]
            mask = valid.rearrange("p (v a b) -> p a v b", a=2, b=2)[:, aa]
            dst = wsel[:, :, :].rearrange("p g (v a b) -> p a g v b", a=2, b=2)[:, aa]
            return (dst, src.rearrange("p g (v b) -> p g v b", b=2),
                    mask.unsqueeze(1).broadcast_to([KROWS, GROUPS, WIN, 2]))

        def plane_rows(kind, py):
            v = planes[:, kind, 2 * py:2 * py + 2, ROW:PLANE - ROW]
            return v.rearrange("c q (m x) -> c q m x", x=PCOL)[:, :, :, 1:1 + WP]

        def plane_bank(kind, py):
            return bank[NAT[kind][py]][:, :].rearrange("c (q m x) -> c q m x", q=2, x=WP)

        NAT = {K: (4, 5), Q: (0, 3), V: (6, 7)}
        CONV = {K: (0, 3), Q: (1, 2), V: (0, 3)}
        KT0, VT0, DEN, TOTAL = (4, 5), (0, 3), 5, 6
        TR = {K: (5, 6), V: (4, 7)}
        SPREAD, VK, M2 = ((4, 7), (1, 2)), ((4, 4, 4, 4), (4, 7, 1, 2)), ((6, 7), (4, 7))
        NATQ = (4, 7)
        FIRST, SECOND = (0, 3, 5, 6), (1, 2, 4, 7)

        def conv_out(kind, half):
            return conv[:, kind, 2 * half:2 * half + 2, :].rearrange("p r n -> p (r n)")

        def tokens(t, pair):
            return t[:, 2 * pair:2 * pair + 2].rearrange("p b t c -> p (b t c)")

        def by_phase(t, pair):
            return t[:, pair].rearrange("p a (h e) -> p h a e", e=E)

        def unbordered(t, py):
            return t[:, :, :].rearrange("c b (p m x) -> c p m b x", p=2, x=WP)[:, py]

        def nat_bank(kind, py):
            return bank[NAT[kind][py]][:, :].rearrange("c (m b x) -> c m b x", b=B, x=WP)

        def v_by_token(pair):
            return (tokens(vt0, pair).rearrange("p (t h e) -> p t e h", e=E, h=HEADS),
                    bank[VT0[pair]][:, :].rearrange("p (t e h) -> p t e h", e=E, h=HEADS))

        def m2_half(a, pair):
            return (m2[a][:, 2 * pair:2 * pair + 2, :].rearrange("p b c -> p (b c)"), bank[M2[a][pair]][:, 0:2 * P])

        def result_parts(b):
            return [slice(0, N)] if b < B - 1 else [slice(0, P), slice(P, N)]

        def tr_bank(i):
            return bank[i][:, :].rearrange("p (h a e) -> p h a e", a=4, e=E)

        block = ctx.enter_context(nc.Block())

        @block.sync
        def _(sp):
            sp.dma_start(wqkv_n[:, :, :], w_qkv.rearrange("(n p) c u v -> p n (c u v)", p=P)).then_inc(ld_wqkv, 16)
            sp.wait_ge(warm_set, 1)
            sp.dma_start(taps_d.rearrange("(p t) -> p t", p=P), warm[:, 0:TFILL]).then_inc(taps_cleared, 16)
            sp.dma_start(wpw_n[:, :, :], w_pw.rearrange("(n p) c u v -> p n (c u v)", p=P)).then_inc(ld_wpw, 16)
            sp.wait_ge(taps_cleared, 16)
            for px in range(2):
                rows = taps_d[px * E * TROW:(px + 1) * E * TROW].rearrange("(c t) -> c t", c=E)
                sp.dma_start(rows[:, TPAD - px:TPAD - px + TLEN].rearrange("c (g t) -> g c t", t=TAPS * TAPS),
                             w_dw.rearrange("(g c) o u v -> g c (o u v)", c=E)).then_inc(taps_in_dram, 16)

            def planes_out(i, py):
                sp.wait_ge((nat_act, nat_dve)[py], i + 1)
                a = slice(2 * py, 2 * py + 2)
                sp.dma_start(planes_d[ORDER[i]][a].rearrange("a p l -> p a l"),
                             planes[:, ORDER[i], a, :]).then_inc(planes_in_dram[ORDER[i]], 16)

            def slots_in(kind, n):
                first, end = CHUNKS[kind][n:n + 2]
                heads = slice(4 * first, 4 * end)
                sp.wait_ge(planes_in_dram[kind], 32)
                src = planes_d[kind].rearrange("a (c g) l -> (a c) g l", c=E)
                for u in range(WIN):
                    sp.dma_start(slots[32 * u:32 * (u + 1), kind, heads, :],
                                 src[:, heads, u * ROW:u * ROW + SLOT]).then_inc(ld_slots[kind, first], 16)

            sp.wait_ge(border_zero, 2)
            planes_out(0, 0)
            planes_out(0, 1)
            sp.wait_ge(taps_in_dram, 32)
            src = bass.AP(taps_d.tensor, taps_d.offset, [[TAPS, 2 * WIN], [TROW, 2 * E], [1, TSPAN]])
            sp.dma_start(taps[:, :], src).then_inc(ld_taps, 16)
            planes_out(1, 0)
            slots_in(K, 0)
            slots_in(K, 1)
            planes_out(1, 1)
            slots_in(K, 2)
            slots_in(K, 3)
            slots_in(Q, 0)
            slots_in(Q, 1)
            for py in range(2):
                sp.wait_ge((nat_act, nat_dve)[py], KINDS)
                for px in range(2):
                    for u in range(WIN):
                        a = 2 * py + px
                        sp.dma_start(slots[32 * u + E * a:32 * u + E * (a + 1), V, :, :],
                                     planes[:, V, a, u * ROW:u * ROW + SLOT]).then_inc(ld_slots[V, 0], 16)
            for b in range(B - 1):
                sp.wait_ge(y_out, b + 1)
                sp.dma_start(out[b].rearrange("c h w -> c (h w)"), ys[:, b, :]).then_inc(stored, 16)
            for half in range(2):
                sp.wait_ge(y_out, B + half)
                pixels = slice(P * half, P * (half + 1))
                sp.dma_start(out[B - 1].rearrange("c h w -> c (h w)")[:, pixels], ys[:, B - 1, pixels]).then_inc(stored, 16)
            sp.wait_ge(stored, 16 * (B + 1))

        @block.gpsimd
        def _(pool):
            nc.gpsimd.memset(ident[:, :], 0.0).then_inc(ident_set, 1)
            pool.wait_ge(ident_set, 1)
            nc.gpsimd.affine_select(out=ident[:, :], in_=ident[:, :], compare_op=ALU.not_equal, fill=1.0,
                                    base=0, pattern=[[-1, P]], channel_multiplier=1).then_inc(ident_set, 1)
            allp = planes[:, :, :, :].rearrange("c k a l -> c (k a) l")
            rows = allp.rearrange("c a (r l) -> c a r l", r=PR)
            nc.gpsimd.memset(rows[:, :, 0:PR:PR - 1, :], 0.0).then_inc(border_zero, 1)
            cols = allp[:, :, ROW:PLANE - ROW].rearrange("c a (m x) -> c a m x", x=PCOL)
            nc.gpsimd.memset(cols[:, :, :, 0:PCOL:PCOL - 1], 0.0).then_inc(border_zero, 1)
            pool.dma_start(consts[:, :], const_in).then_inc(ld_const, 16)
            nc.gpsimd.memset(pick_b[:, :, :, :].bitcast(F32), 0.0).then_inc(pick_zero, 1)
            pool.dma_start(bth[:, :], b_theta.rearrange("(p o) -> p o", o=1)).then_inc(ld_bias, 16)
            pool.dma_start(bph[:, :], b_phi.rearrange("(p o) -> p o", o=1)).then_inc(ld_bias, 16)
            pool.dma_start(bfu[:, :], b_fuse.rearrange("(p o) -> p o", o=1)).then_inc(ld_bias, 16)
            pool.wait_ge(ld_const, 16)
            pool.wait_ge(ld_taps, 16)
            nc.gpsimd.tensor_tensor(*selected_taps(0), ALU.mult).then_inc(wsel_pool, 1)
            pool.wait_ge(pick_zero, 1)
            for b in range(B):
                rows = slice(32 * b, 32 * (b + 1))
                if b:
                    pool.wait_ge(pick_set, b)
                nc.gpsimd.tensor_copy(pick_b[rows, b], pick[rows]).then_inc(pick_set, 1)
            pool.wait_ge(pick_set, B)
            pool.wait_ge(wsel_pool, 1)
            pool.wait_ge(wsel_dve, 1)
            pool.wait_ge(wpw_out, 1)
            for kind in (Q, V):
                nc.gpsimd.tensor_tensor(*conv_weights(kind, slice(0, HEADS)), ALU.mult).then_inc(wconv_pool, 1)

        @block.scalar
        def _(act):
            act.dma_start(xs[:, :, :], x.rearrange("b c h w -> c b (h w)")).then_inc(ld_x, 16)
            act.dma_start(wproj_n[:, :], w_proj.rearrange("o c u v -> o (c u v)")).then_inc(ld_wproj, 16)
            act.dma_start(wfuse_n[:, :], w_fuse).then_inc(ld_wl1, 16)
            act.dma_start(wth_n[:, :], w_theta).then_inc(ld_wl1, 16)
            act.dma_start(wph_n[:, :], w_phi).then_inc(ld_wl1, 16)
            act.wait_ge(ld_wpw, 16)
            nc.scalar.activation(wpw_r[:, :, :, :], wpw_n[:, :, :].unsqueeze(2).broadcast_to([P, KINDS, WIN * 4, E]),
                                 ACT.Copy).then_inc(wpw_copied, 1)

            def plain_key_sums(images):
                act.wait_ge(kn_act, 1)
                act.wait_ge(kn_dve, 1)
                for b in images:
                    if b:
                        act.wait_ge(ks0_sum, b)
                    nc.scalar.activation(k_copy[:, :], kn[:, b, :], ACT.Copy, accum_out=ksum0[:, b:b + 1]).then_inc(ks0_sum, 1)

            for i, kind in enumerate(ORDER):
                act.wait_ge(nat_mm, 2 * i + 1)
                if kind != V:
                    nc.scalar.activation(plane_rows(kind, 0), plane_bank(kind, 0), ACT.Copy).then_inc(nat_act, 1)
                if kind == K:
                    nc.scalar.activation(unbordered(kn, 0), nat_bank(K, 0), ACT.Relu).then_inc(kn_act, 1)
                if kind == Q:
                    for px in range(2):
                        nc.scalar.activation(parity(rq[0], 0, px), split(NAT[Q][0])[:, px], ACT.Relu).then_inc(rq0_act, 1)
                    plain_key_sums((0, 1))
                if kind == V:
                    nc.scalar.activation(unbordered(vn, 0), nat_bank(V, 0), ACT.Copy).then_inc(vn_act, 1)
                    plain_key_sums((2, 3))
            for pair in range(2):
                act.wait_ge(kt0_mm, pair + 1)
                nc.scalar.activation(tokens(kt0, pair), bank[KT0[pair]][:, :], ACT.Copy).then_inc(kt0_out, 1)
            nc.scalar.activation(plane_rows(V, 0), plane_bank(V, 0), ACT.Copy).then_inc(nat_act, 1)
            act.wait_ge(vt0_mm, 2)
            nc.scalar.activation(*v_by_token(1), ACT.Copy).then_inc(vt0_act, 1)
            act.wait_ge(wpr_mm, 1)
            nc.scalar.activation(wproj_t[:, :, :].rearrange("p a c -> p (a c)"), bank[1][:, 0:2 * P], ACT.Copy).then_inc(wpr_out, 1)
            act.wait_ge(wl1_mm, 1)
            nc.scalar.activation(wfuse_t[:, :], bank[2][:, 0:C], ACT.Copy).then_inc(wl1_out, 1)
            nc.scalar.activation(wtp_t[:, :], bank[2][:, C:C + 2 * D], ACT.Copy).then_inc(wl1_out, 1)
            for pair in range(2):
                act.wait_ge(m2_mm[0], pair + 1)
                nc.scalar.activation(*m2_half(0, pair), ACT.Copy).then_inc(m2_out[0], 1)
            for i, kind in enumerate(ORDER):
                act.wait_ge(conv_mm, 2 * i + 1)
                nc.scalar.activation(conv_out(kind, 0), bank[CONV[kind][0]][:, :],
                                     ACT.Relu if kind == K else ACT.Copy).then_inc(conv_act, 1)
                if kind == Q:
                    for pair in range(2):
                        act.wait_ge(tr_k_mm, pair + 1)
                        nc.scalar.activation(by_phase(kt1, pair), tr_bank(TR[K][pair]), ACT.Copy).then_inc(kt1_out, 1)
                    act.wait_ge(natq_mm, 1)
                    for bb in range(2):
                        nc.scalar.activation(parity(rq[1], 1, 1 - bb, "b y x"), split(NATQ[0], "b y x")[:, bb],
                                             ACT.Relu).then_inc(rq1_act, 1)
            act.wait_ge(tr_v_mm, 1)
            nc.scalar.activation(by_phase(vt1, 0), tr_bank(TR[V][0]), ACT.Copy).then_inc(vt1_act, 1)
            act.wait_ge(m2_mm[1], 1)
            nc.scalar.activation(*m2_half(1, 0), ACT.Copy).then_inc(m2_out[1], 1)
            act.wait_ge(ld_bias, 48)
            act.wait_ge(bias_scaled, 1)

            def theta_phi(b):
                act.wait_ge(tf_mm, b + 1)
                src = bank[SECOND[b]]
                nc.scalar.activation(theta[:, b, :], src[0:D, 0:N], ACT.Identity, bias=bth_s[:, 0:1],
                                     scale=D ** -0.5).then_inc(tp_out, 1)
                nc.scalar.activation(phi[:, b, :], src[D:2 * D, 0:N], ACT.Identity, bias=bph[:, 0:1]).then_inc(tp_out, 1)

            def values(b):
                act.wait_ge(tf_mm, b + 1)
                nc.scalar.activation(gf[:, b].rearrange("p k c -> p (k c)"), bank[SECOND[b]][:, N:2 * N],
                                     ACT.Copy).then_inc(gf_out[b], 1)

            def exponentials(b):
                act.wait_ge(nmx_out, b + 1)
                for qc in range(2):
                    nc.scalar.activation(pr[:, b, qc, :], bank[FIRST[b]][:, qc * N:(qc + 1) * N], ACT.Exp,
                                         bias=nmx[:, b, qc:qc + 1],
                                         accum_out=rs[:, b, qc:qc + 1]).then_inc(exp_out, 1)

            def transposed(b):
                act.wait_ge(pt_mm, b + 1)
                nc.scalar.activation(pt[:, b].rearrange("p k n -> p (k n)"), bank[SECOND[b]][:, :], ACT.Copy).then_inc(pt_out[b], 1)

            for step, b in ((theta_phi, 0), (values, 0), (theta_phi, 1), (theta_phi, 2), (exponentials, 0),
                            (theta_phi, 3), (exponentials, 1), (exponentials, 2), (transposed, 0), (values, 2),
                            (exponentials, 3), (values, 3), (transposed, 2), (transposed, 3)):
                step(b)

        @block.vector
        def _(dve):
            nc.vector.memset(warm[:, :], 0.0).then_inc(warm_set, 1)
            dve.wait_ge(wt_mm, 1)
            src = bank[1][:, 0:KINDS * P].rearrange("c (h k e) -> c k e h", k=KINDS, e=E)
            for kind in ORDER:
                nc.vector.tensor_copy(wqkv_t[:, kind].rearrange("c (e h) -> c e h", e=E), src[:, kind]).then_inc(wt_out, 1)
            for i, kind in enumerate(ORDER):
                dve.wait_ge(nat_mm, 2 * i + 2)
                if kind == V:
                    nc.vector.tensor_copy(unbordered(vn, 1), nat_bank(V, 1)).then_inc(vn_dve, 1)
                nc.vector.tensor_copy(plane_rows(kind, 1), plane_bank(kind, 1)).then_inc(nat_dve, 1)
                if kind == K:
                    nc.vector.tensor_scalar_max(unbordered(kn, 1), nat_bank(K, 1), 0.0).then_inc(kn_dve, 1)
                if kind == Q:
                    for px in range(2):
                        nc.vector.tensor_scalar_max(parity(rq[0], 1, px), split(NAT[Q][1])[:, px], 0.0).then_inc(rq0_dve, 1)
                    dve.wait_ge(wpw_mm, 1)
                    nc.vector.tensor_copy(wpw_t[:, :], bank[2][0:KROWS, 0:GROUPS * E]).then_inc(wpw_out, 1)

            def key_sums(a, sums):
                shape = [P, B, 2, HEADS] if a == 0 else [P, B, HEADS, 2]
                if a == 0:
                    mask = same[0][:, 0:32].rearrange("p (t h) -> p t h", t=2)
                    dst = ks[0][:, :, :].rearrange("p b (t h) -> p b t h", t=2)
                else:
                    mask = same[1].rearrange("p (h e) -> p h e", e=E)[:, :, 0:2]
                    dst = ks[1][:, :, :].rearrange("p b (h t) -> p b h t", t=2)
                nc.vector.tensor_tensor(dst, sums.unsqueeze(2).unsqueeze(3).broadcast_to(shape),
                                        mask.unsqueeze(1).broadcast_to(shape), ALU.mult).then_inc(ks_out[a], 1)

            dve.wait_ge(ld_const, 16)
            dve.wait_ge(ks0_sum, B)
            key_sums(0, ksum0[:, :])
            dve.wait_ge(ld_taps, 16)
            nc.vector.tensor_tensor(*selected_taps(1), ALU.mult).then_inc(wsel_dve, 1)
            dve.wait_ge(vt0_mm, 1)
            nc.vector.tensor_copy(*v_by_token(0)).then_inc(vt0_dve, 1)
            dve.wait_ge(wsel_pool, 1)
            dve.wait_ge(wsel_dve, 1)
            dve.wait_ge(wpw_out, 1)
            nc.vector.tensor_tensor(*conv_weights(K, slice(0, 8)), ALU.mult).then_inc(wconv_dve, 1)

            def attend_sums(a, b):
                dve.wait_ge(vk_mm[a], b + 1 if a else 1)
                if a == 0:
                    shape = [P, E, HEADS // 4, 4]
                    src = bank[VK[0][b]][:, 32 * b:32 * (b + 1)].rearrange("p (e m) -> p e m", m=4)
                    nc.vector.tensor_tensor(vk[0][:, b, :].rearrange("p (e j m) -> p e j m", j=HEADS // 4, m=4),
                                            src.unsqueeze(2).broadcast_to(shape),
                                            cross.rearrange("p (e j m) -> p e j m", j=HEADS // 4, m=4),
                                            ALU.mult).then_inc(vk_out[0], 1)
                else:
                    nc.vector.tensor_tensor(vk[1][:, b, :].rearrange("p (j m) -> p j m", m=32),
                                            bank[VK[1][b]][:, 0:32].unsqueeze(1).broadcast_to([P, HEADS // 4, 32]),
                                            same[1].rearrange("p (j m) -> p j m", m=32), ALU.mult).then_inc(vk_out[1], 1)

            def reciprocals(a):
                dve.wait_ge(den_mm[a], 1)
                nc.vector.tensor_scalar_add(den[a][:, :], bank[DEN][:, 0:N], EPS).then_inc(den_out[a], 1)
                dve.wait_ge(den_out[a], 1)
                nc.vector.reciprocal(rden[a][:, :], den[a][:, :]).then_inc(rden_out[a], 1)
                dve.wait_ge(rden_out[a], 1)
                nc.vector.tensor_copy(rden_hi[:, :], rden[a][:, :]).then_inc(rden_split[a], 1)
                dve.wait_ge(rden_split[a], 1)
                nc.vector.tensor_tensor(rden_lo[:, :], rden[a][:, :], rden_hi[:, :].bitcast(F32),
                                        ALU.subtract).then_inc(rden_split[a], 1)

            def scale_q(a, pair):
                dve.wait_ge(bc_mm[a], pair + 1)
                o = qs[a][:, 2 * pair:2 * pair + 2, :].rearrange("p b n -> p (b n)")
                q = rq[a][:, 2 * pair:2 * pair + 2, :].rearrange("p b n -> p (b n)")
                nc.vector.tensor_tensor(o, bank[SPREAD[a][pair]][:, :], q, ALU.mult).then_inc(qs_out[a], 1)

            def conv_last_rounds(i):
                kind = ORDER[i]
                dve.wait_ge(conv_mm, 2 * i + 2)
                if kind == K:
                    nc.vector.tensor_scalar_max(conv_out(kind, 1), bank[CONV[kind][1]][:, :], 0.0).then_inc(conv_dve, 1)
                else:
                    nc.vector.tensor_copy(conv_out(kind, 1), bank[CONV[kind][1]][:, :]).then_inc(conv_dve, 1)

            for b in range(B):
                attend_sums(0, b)
            nc.vector.tensor_tensor(*conv_weights(K, slice(8, HEADS)), ALU.mult).then_inc(wconv_dve, 1)
            reciprocals(0)
            conv_last_rounds(0)
            for half in range(2):
                dve.wait_ge((conv_act, conv_dve)[half], 1)
                src = conv[:, K, 2 * half:2 * half + 2, :].rearrange("p r (b n) -> p r b n", b=B)
                nc.vector.tensor_reduce(ksum1[:, 2 * half:2 * half + 2, :], src, AX_X, ALU.add).then_inc(ks1_sum, 1)
            scale_q(0, 0)
            scale_q(0, 1)
            conv_last_rounds(1)
            dve.wait_ge(natq_mm, 2)
            for bb in range(2):
                nc.vector.tensor_scalar_max(parity(rq[1], 0, 1 - bb, "b y x"), split(NATQ[1], "b y x")[:, bb],
                                            0.0).then_inc(rq1_dve, 1)
            dve.wait_ge(tot_mm, 1)
            key_sums(1, bank[TOTAL][:, 0:B])
            reciprocals(1)
            conv_last_rounds(2)
            scale_q(1, 0)
            scale_q(1, 1)
            dve.wait_ge(tr_v_mm, 2)
            nc.vector.tensor_copy(by_phase(vt1, 1), tr_bank(TR[V][1])).then_inc(vt1_dve, 1)
            for b in range(B):
                attend_sums(1, b)
            dve.wait_ge(m2_mm[1], 2)
            nc.vector.tensor_copy(*m2_half(1, 1)).then_inc(m2_last_out, 1)

            def first_layer(b):
                dve.wait_ge(proj_mm, b + 1)
                nc.vector.tensor_tensor(x1[:, b, :], bank[FIRST[b]][:, 0:N], xs[:, b, :], ALU.add).then_inc(x1_out, 1)

            def maxima(b):
                dve.wait_ge(f_mm, b + 1)
                nc.vector.tensor_reduce(nmx[:, b, :], bank[FIRST[b]][:, :].rearrange("p (q n) -> p q n", q=2),
                                        AX_X, ALU.max, negate=True).then_inc(nmx_out, 1)

            def values(b):
                dve.wait_ge(tp_out, 2 * b + 2)
                nc.vector.tensor_copy(gf[:, b].rearrange("p k c -> p (k c)"),
                                      bank[SECOND[b]][:, N:2 * N]).then_inc(gf_out[b], 1)

            def normalize(b):
                dve.wait_ge(exp_out, 2 * b + 2)
                nc.vector.reciprocal(rrs[:, b, :], rs[:, b, :]).then_inc(rrs_out, 1)
                dve.wait_ge(rrs_out, b + 1)
                for qc in range(2):
                    nc.vector.tensor_scalar_mul(pn[:, b, qc, :], pr[:, b, qc, :], rrs[:, b, qc:qc + 1]).then_inc(pn_out, 1)

            def transposed(b):
                dve.wait_ge(pt_mm, b + 1)
                nc.vector.tensor_copy(pt[:, b].rearrange("p k n -> p (k n)"), bank[SECOND[b]][:, :]).then_inc(pt_out[b], 1)

            def result(b):
                for n, pixels in enumerate(result_parts(b)):
                    dve.wait_ge(y_mm, b + 1 + n)
                    src = bank[(FIRST[b], SECOND[b])[n]][:, pixels]
                    nc.vector.scalar_tensor_tensor(ys[:, b, pixels], src, bfu[:, 0:1], x1[:, b, pixels],
                                                   ALU.add, ALU.add).then_inc(y_out, 1)

            dve.wait_ge(ld_bias, 48)
            nc.vector.tensor_scalar_mul(bth_s[:, :], bth[:, :], D ** -0.5).then_inc(bias_scaled, 1)
            for step, b in ((first_layer, 0), (first_layer, 1), (first_layer, 2), (first_layer, 3), (maxima, 0),
                            (maxima, 1), (normalize, 0), (maxima, 2), (values, 1), (normalize, 1), (maxima, 3),
                            (normalize, 2), (transposed, 1), (normalize, 3), (result, 0), (result, 1),
                            (result, 2), (result, 3)):
                step(b)

        @block.tensor
        def _(pe):
            pe.wait_ge(warm_set, 1)

            def keep_warm(n):
                for _ in range(n):
                    nc.tensor.matmul(bank[3][:, 0:N], warm[:, 0:P], warm[:, :], start=True, stop=True)

            keep_warm(2)
            pe.wait_ge(ld_wqkv, 16)
            pe.wait_ge(ident_set, 2)
            for n in range(KINDS):
                last = nc.tensor.transpose(bank[1][:, n * P:(n + 1) * P], wqkv_n[:, n, :], ident[:, :])
            last.then_inc(wt_mm, 1)
            keep_warm(1)
            pe.wait_ge(ld_x, 16)

            def natural(i):
                kind = ORDER[i]
                pe.wait_ge(wt_out, i + 1)
                for py in range(2):
                    for px in range(2):
                        last = nc.tensor.matmul(bank[NAT[kind][py]][:, px * NPIX:(px + 1) * NPIX],
                                                wqkv_t[:, kind, :], parity(xs, py, px), start=True, stop=True)
                    last.then_inc(nat_mm, 1)

            natural(0)
            natural(1)
            pe.wait_ge(wpw_copied, 1)
            for n in range(KINDS):
                src = wpw_r[:, n].rearrange("p s e -> p (s e)")
                last = nc.tensor.transpose(bank[2][0:KROWS, n * P:(n + 1) * P], src, ident[:, :])
            last.then_inc(wpw_mm, 1)
            natural(2)
            pe.wait_ge(ld_wproj, 16)
            nc.tensor.transpose(bank[1][:, 0:P], wproj_n[:, 0:P], ident[:, :])
            nc.tensor.transpose(bank[1][:, P:2 * P], wproj_n[:, P:2 * P], ident[:, :]).then_inc(wpr_mm, 1)

            def plain_tokens(t, banks, done):
                for pair in range(2):
                    for n in range(4):
                        b, py = 2 * pair + n // 2, n % 2
                        last = nc.tensor.transpose(bank[banks[pair]][:, n * P:(n + 1) * P],
                                                   t[:, b, py * P:(py + 1) * P], ident[:, :])
                    last.then_inc(done, 1)

            pe.wait_ge(kn_act, 1)
            pe.wait_ge(kn_dve, 1)
            plain_tokens(kn, KT0, kt0_mm)
            pe.wait_ge(ld_wl1, 48)
            pe.wait_ge(wpw_out, 1)
            nc.tensor.transpose(bank[2][:, 0:C], wfuse_n[:, :], ident[:, :])
            nc.tensor.transpose(bank[2][:, C:C + D], wth_n[:, :], ident[0:D, 0:D])
            nc.tensor.transpose(bank[2][:, C + D:C + 2 * D], wph_n[:, :], ident[0:D, 0:D]).then_inc(wl1_mm, 1)
            pe.wait_ge(vn_act, 1)
            pe.wait_ge(vn_dve, 1)
            pe.wait_ge(rq0_act, 2)
            pe.wait_ge(rq0_dve, 2)
            plain_tokens(vn, VT0, vt0_mm)

            def denominators(a):
                pe.wait_ge(ks_out[a], 1)
                if a == 1:
                    pe.wait_ge(rq1_act, 2)
                    pe.wait_ge(rq1_dve, 2)
                for b in range(B):
                    last = nc.tensor.matmul(bank[DEN][32 * b:32 * (b + 1), 0:N], ks[a][:, b, :], rq[a][:, b, :],
                                            start=True, stop=True)
                last.then_inc(den_mm[a], 1)

            def projected_sums(a):
                for pair in range(2):
                    for s in range(2):
                        pe.wait_ge(vk_out[a], 2 * pair + s + 1)
                        last = nc.tensor.matmul(bank[M2[a][pair]][:, s * P:(s + 1) * P], vk[a][:, 2 * pair + s, :],
                                                wproj_t[:, a, :], start=True, stop=True)
                    last.then_inc(m2_mm[a], 1)

            def spread(a, pair):
                pe.wait_ge(rden_split[a], 2)
                pe.wait_ge(pick_set, B)
                for s in range(2):
                    b = 2 * pair + s
                    dst = bank[SPREAD[a][pair]][:, s * N:(s + 1) * N]
                    nc.tensor.matmul(dst, pick_b[:, b, a, :], rden_hi[:, :], start=True, stop=False)
                    last = nc.tensor.matmul(dst, pick_b[:, b, a, :], rden_lo[:, :], start=False, stop=True)
                last.then_inc(bc_mm[a], 1)

            def convolve(i, r):
                kind = ORDER[i]
                if (kind, r) in ld_slots:
                    pe.wait_ge(ld_slots[kind, r], 16 * WIN * (4 if kind == V else 1))
                dst = bank[CONV[kind][r // 2]]
                at = r % 2 * NPIX
                for v in range(WIN):
                    for j in range(4):
                        h = 4 * r + j
                        w = wconv[:, kind, h, 4 * v:4 * (v + 1), :].rearrange("p a o -> p (a o)")
                        src = slots[:, kind, h, :].rearrange("p (y b x) -> p b y x", b=B, x=PCOL)[:, :, :, v:v + WP]
                        last = nc.tensor.matmul(dst[32 * j:32 * (j + 1), at:at + NPIX], w, src,
                                                start=v == 0, stop=v == WIN - 1)
                if r % 2:
                    last.then_inc(conv_mm, 1)

            def by_token(kind, pair, done):
                for r in range(4):
                    src = conv[:, kind, r, pair * P:(pair + 1) * P]
                    last = nc.tensor.transpose(bank[TR[kind][pair]][:, r * P:(r + 1) * P], src, ident[:, :])
                last.then_inc(done, 1)

            pe.wait_ge(kt0_out, 2)
            denominators(0)
            pe.wait_ge(vt0_dve, 1)
            pe.wait_ge(vt0_act, 1)
            for b in range(B):
                for t in range(2):
                    for j in range(4):
                        k4 = kt0[:, b, t, :].rearrange("p (e h) -> p e h", e=E)[:, :, 4 * j:4 * j + 4]
                        dst = bank[VK[0][0]][32 * j:32 * (j + 1), 32 * b:32 * (b + 1)]
                        last = nc.tensor.matmul(dst, vt0[:, b, t, 32 * j:32 * (j + 1)], k4, start=t == 0, stop=t == 1)
            last.then_inc(vk_mm[0], 1)
            pe.wait_ge(wconv_dve, 1)
            convolve(0, 0)
            convolve(0, 1)
            pe.wait_ge(wpr_out, 1)
            pe.wait_ge(nat_act, KINDS)
            pe.wait_ge(nat_dve, KINDS)
            projected_sums(0)
            pe.wait_ge(wconv_dve, 2)
            convolve(0, 2)
            convolve(0, 3)
            spread(0, 0)
            pe.wait_ge(m2_out[0], 2)
            spread(0, 1)
            pe.wait_ge(wconv_pool, 1)
            convolve(1, 0)
            convolve(1, 1)
            pe.wait_ge(wl1_out, 2)
            convolve(1, 2)
            convolve(1, 3)
            pe.wait_ge(conv_act, 1)
            pe.wait_ge(conv_dve, 1)
            by_token(K, 0, tr_k_mm)
            by_token(K, 1, tr_k_mm)
            pe.wait_ge(conv_act, 2)
            pe.wait_ge(conv_dve, 2)
            pe.wait_ge(qs_out[0], 2)
            for aa in range(2):
                for bb in range(2):
                    w = gather[:, 32 * (2 * aa + bb):32 * (2 * aa + bb + 1)]
                    for r in range(4):
                        last = nc.tensor.matmul(bank[NATQ[aa]][32 * r:32 * (r + 1), bb * NPIX:(bb + 1) * NPIX], w,
                                                conv[:, Q, r, :], start=True, stop=True)
                last.then_inc(natq_mm, 1)
            pe.wait_ge(kt1_out, 2)
            pe.wait_ge(ks1_sum, 2)
            for r in range(4):
                last = nc.tensor.matmul(bank[TOTAL][32 * r:32 * (r + 1), 0:B], total, ksum1[:, r, :],
                                        start=True, stop=True)
            last.then_inc(tot_mm, 1)
            pe.wait_ge(wconv_pool, 2)
            convolve(2, 0)
            denominators(1)
            convolve(2, 1)
            convolve(2, 2)
            convolve(2, 3)
            spread(1, 0)
            spread(1, 1)
            pe.wait_ge(conv_act, 3)
            pe.wait_ge(conv_dve, 3)
            by_token(V, 0, tr_v_mm)
            by_token(V, 1, tr_v_mm)

            def project(b, a):
                if a == 0:
                    pe.wait_ge(den_out[1], 1)
                    pe.wait_ge(ks_out[1], 1)
                else:
                    pe.wait_ge((m2_out[1], m2_last_out)[b // 2], 1)
                    pe.wait_ge(qs_out[1], b // 2 + 1)
                last = nc.tensor.matmul(bank[FIRST[b]][:, 0:N], m2[a][:, b, :], qs[a][:, b, :],
                                        start=a == 0, stop=a == 1)
                if a == 1:
                    last.then_inc(proj_mm, 1)

            def theta_phi_values(b):
                pe.wait_ge(x1_out, b + 1)
                dst = bank[SECOND[b]]
                nc.tensor.matmul(dst[:, 0:N], wtp_t[:, :], x1[:, b, :], start=True, stop=True)
                for kc in range(2):
                    last = nc.tensor.matmul(dst[:, N + kc * C:N + (kc + 1) * C], x1[:, b, kc * P:(kc + 1) * P],
                                            wfuse_t[:, :], start=True, stop=True)
                last.then_inc(tf_mm, 1)

            def scores(b):
                pe.wait_ge(tp_out, 2 * b + 2)
                for qc in range(2):
                    last = nc.tensor.matmul(bank[FIRST[b]][:, qc * N:(qc + 1) * N], theta[:, b, qc * P:(qc + 1) * P],
                                            phi[:, b, :], start=True, stop=True)
                last.then_inc(f_mm, 1)

            def transpose_probs(b):
                pe.wait_ge(pn_out, 2 * b + 2)
                pe.wait_ge(gf_out[b], 1)
                for kc in range(2):
                    for qc in range(2):
                        at = kc * N + qc * P
                        last = nc.tensor.transpose(bank[SECOND[b]][:, at:at + P], pn[:, b, qc, kc * P:(kc + 1) * P], ident[:, :])
                last.then_inc(pt_mm, 1)

            def attend(b):
                pe.wait_ge(pt_out[b], 1)
                for n, pixels in enumerate(result_parts(b)):
                    dst = bank[(FIRST[b], SECOND[b])[n]][:, pixels]
                    for kc in range(2):
                        last = nc.tensor.matmul(dst, gf[:, b, kc, :], pt[:, b, kc, pixels], start=kc == 0, stop=kc == 1)
                    last.then_inc(y_mm, 1)

            project(0, 0)
            project(1, 0)
            pe.wait_ge(vt1_act, 1)
            pe.wait_ge(vt1_dve, 1)
            for b in range(B):
                if b >= 2:
                    pe.wait_ge(qs_out[1], b - 1)
                pair, rows = b // 2, slice(D * (b % 2), D * (b % 2 + 1))
                for ph in range(4):
                    for j in range(4):
                        cols = slice(32 * j, 32 * (j + 1))
                        last = nc.tensor.matmul(bank[VK[1][b]][cols, 0:32], vt1[rows, pair, ph, cols],
                                                kt1[rows, pair, ph, cols], start=ph == 0, stop=ph == 3)
                last.then_inc(vk_mm[1], 1)
            projected_sums(1)
            project(2, 0)
            project(3, 0)
            for b in range(B):
                project(b, 1)
            for step, b in ((theta_phi_values, 0), (theta_phi_values, 1), (theta_phi_values, 2), (scores, 0),
                            (scores, 1), (theta_phi_values, 3), (scores, 2), (scores, 3), (transpose_probs, 0),
                            (transpose_probs, 1), (attend, 0), (transpose_probs, 2), (attend, 1),
                            (transpose_probs, 3), (attend, 2), (attend, 3)):
                step(b)


_INS = ["x", "L0_conv_w_qkv", "L0_conv_w_dw", "L0_conv_w_pw", "L0_conv_w_proj", "L1_conv_W_theta",
        "L1_conv_b_theta", "L1_conv_W_phi", "L1_conv_b_phi", "L1_conv_W_fuse", "L1_conv_b_fuse"]


def kernel(**inputs):
    import concourse.bacc as bacc
    from concourse.bass_utils import run_bass_kernel_spmd

    nc = bacc.Bacc("TRN2", target_bir_lowering=False, num_devices=1)
    arrays = {n: np.ascontiguousarray(inputs[n]) for n in _INS}
    arrays["shape_constants"] = shape_constants()
    args, in_map = [], {}
    for name, a in arrays.items():
        in_map[f"in_{name}"] = a
        args.append(nc.dram_tensor(f"in_{name}", a.shape, mybir.dt.from_np(a.dtype), kind="ExternalInput").ap())
    out = nc.dram_tensor("out_0", (B, C, H, W), F32, kind="ExternalOutput").ap()
    conv_attention_kernel(nc, *args, out)
    r = run_bass_kernel_spmd(nc, [in_map], core_ids=[0])
    return r.results[0]["out_0"]
```
